# Optimizing a Trainium2 kernel written in Bass

```python
import numpy as np
import jax
import jax.numpy as jnp

def _softmax(x, axis=-1):
    return jax.nn.softmax(x, axis=axis)

def _gelu(x):
    return jax.nn.gelu(x, approximate=True)

def _silu(x):
    return jax.nn.silu(x)

def _sigmoid(x):
    return jax.nn.sigmoid(x)

def _layernorm(x, axis=-1, eps=1e-05):
    m = jnp.mean(x, axis=axis, keepdims=True)
    v = jnp.var(x, axis=axis, keepdims=True)
    return (x - m) / jnp.sqrt(v + eps)

def _scatter_add(tgt, idx, src, axis=0):
    return tgt.at[idx].add(src)

def _segment_sum(src, seg, n):
    return jax.ops.segment_sum(src, seg, n)
kernel_name = 'mk_dlrm_tower_d1_rec_r8_c673d0'

def setup_inputs(seed: int=0):
    np.random.seed(seed)
    _w = jnp.asarray

    def _rec_inputs():
        import jax
        import jax.numpy as jnp
        _tk = jax.random.key(seed)
        dense_ctx = jax.random.normal(jax.random.fold_in(_tk, 190), (1024, 16), jnp.float32)
        ids = jnp.stack([jax.random.randint(jax.random.fold_in(_tk, 200 + f), (1024,), 0, v, jnp.int32) for f, v in enumerate([1250, 125000, 1000, 1000, 1250, 1000, 1250, 1000, 1250, 1250, 1250, 12500, 125000, 1250, 1250, 1000, 12500, 1250, 1250, 125000, 1000, 1250, 1000, 12500, 1000, 1000, 1250, 1250, 12500, 1000, 1000, 12500])], axis=1)
        tbl_0 = 0.05 * jax.random.normal(jax.random.fold_in(_tk, 500 + 0), (1250, 64), jnp.float32)
        tbl_1 = 0.05 * jax.random.normal(jax.random.fold_in(_tk, 500 + 1), (125000, 64), jnp.float32)
        tbl_2 = 0.05 * jax.random.normal(jax.random.fold_in(_tk, 500 + 2), (1000, 64), jnp.float32)
        tbl_3 = 0.05 * jax.random.normal(jax.random.fold_in(_tk, 500 + 3), (1000, 64), jnp.float32)
        tbl_4 = 0.05 * jax.random.normal(jax.random.fold_in(_tk, 500 + 4), (1250, 64), jnp.float32)
        tbl_5 = 0.05 * jax.random.normal(jax.random.fold_in(_tk, 500 + 5), (1000, 64), jnp.float32)
        tbl_6 = 0.05 * jax.random.normal(jax.random.fold_in(_tk, 500 + 6), (1250, 64), jnp.float32)
        tbl_7 = 0.05 * jax.random.normal(jax.random.fold_in(_tk, 500 + 7), (1000, 64), jnp.float32)
        tbl_8 = 0.05 * jax.random.normal(jax.random.fold_in(_tk, 500 + 8), (1250, 64), jnp.float32)
        tbl_9 = 0.05 * jax.random.normal(jax.random.fold_in(_tk, 500 + 9), (1250, 64), jnp.float32)
        tbl_10 = 0.05 * jax.random.normal(jax.random.fold_in(_tk, 500 + 10), (1250, 64), jnp.float32)
        tbl_11 = 0.05 * jax.random.normal(jax.random.fold_in(_tk, 500 + 11), (12500, 64), jnp.float32)
        tbl_12 = 0.05 * jax.random.normal(jax.random.fold_in(_tk, 500 + 12), (125000, 64), jnp.float32)
        tbl_13 = 0.05 * jax.random.normal(jax.random.fold_in(_tk, 500 + 13), (1250, 64), jnp.float32)
        tbl_14 = 0.05 * jax.random.normal(jax.random.fold_in(_tk, 500 + 14), (1250, 64), jnp.float32)
        tbl_15 = 0.05 * jax.random.normal(jax.random.fold_in(_tk, 500 + 15), (1000, 64), jnp.float32)
        tbl_16 = 0.05 * jax.random.normal(jax.random.fold_in(_tk, 500 + 16), (12500, 64), jnp.float32)
        tbl_17 = 0.05 * jax.random.normal(jax.random.fold_in(_tk, 500 + 17), (1250, 64), jnp.float32)
        tbl_18 = 0.05 * jax.random.normal(jax.random.fold_in(_tk, 500 + 18), (1250, 64), jnp.float32)
        tbl_19 = 0.05 * jax.random.normal(jax.random.fold_in(_tk, 500 + 19), (125000, 64), jnp.float32)
        tbl_20 = 0.05 * jax.random.normal(jax.random.fold_in(_tk, 500 + 20), (1000, 64), jnp.float32)
        tbl_21 = 0.05 * jax.random.normal(jax.random.fold_in(_tk, 500 + 21), (1250, 64), jnp.float32)
        tbl_22 = 0.05 * jax.random.normal(jax.random.fold_in(_tk, 500 + 22), (1000, 64), jnp.float32)
        tbl_23 = 0.05 * jax.random.normal(jax.random.fold_in(_tk, 500 + 23), (12500, 64), jnp.float32)
        tbl_24 = 0.05 * jax.random.normal(jax.random.fold_in(_tk, 500 + 24), (1000, 64), jnp.float32)
        tbl_25 = 0.05 * jax.random.normal(jax.random.fold_in(_tk, 500 + 25), (1000, 64), jnp.float32)
        tbl_26 = 0.05 * jax.random.normal(jax.random.fold_in(_tk, 500 + 26), (1250, 64), jnp.float32)
        tbl_27 = 0.05 * jax.random.normal(jax.random.fold_in(_tk, 500 + 27), (1250, 64), jnp.float32)
        tbl_28 = 0.05 * jax.random.normal(jax.random.fold_in(_tk, 500 + 28), (12500, 64), jnp.float32)
        tbl_29 = 0.05 * jax.random.normal(jax.random.fold_in(_tk, 500 + 29), (1000, 64), jnp.float32)
        tbl_30 = 0.05 * jax.random.normal(jax.random.fold_in(_tk, 500 + 30), (1000, 64), jnp.float32)
        tbl_31 = 0.05 * jax.random.normal(jax.random.fold_in(_tk, 500 + 31), (12500, 64), jnp.float32)
        _rk = jax.random.fold_in(_tk, 7)
        W_top1 = 0.0693375 * jax.random.normal(jax.random.fold_in(_tk, 801), (208, 512), jnp.float32)
        W_top2 = 0.0441942 * jax.random.normal(jax.random.fold_in(_tk, 802), (512, 256), jnp.float32)
        W_top3 = 0.0625 * jax.random.normal(jax.random.fold_in(_tk, 803), (256, 1), jnp.float32)
        b_top1 = jnp.zeros((512,), jnp.float32)
        b_top2 = jnp.zeros((256,), jnp.float32)
        return (dense_ctx, ids, tbl_0, tbl_1, tbl_2, tbl_3, tbl_4, tbl_5, tbl_6, tbl_7, tbl_8, tbl_9, tbl_10, tbl_11, tbl_12, tbl_13, tbl_14, tbl_15, tbl_16, tbl_17, tbl_18, tbl_19, tbl_20, tbl_21, tbl_22, tbl_23, tbl_24, tbl_25, tbl_26, tbl_27, tbl_28, tbl_29, tbl_30, tbl_31, W_top1, b_top1, W_top2, b_top2, W_top3)
    dense_ctx, ids, tbl_0, tbl_1, tbl_2, tbl_3, tbl_4, tbl_5, tbl_6, tbl_7, tbl_8, tbl_9, tbl_10, tbl_11, tbl_12, tbl_13, tbl_14, tbl_15, tbl_16, tbl_17, tbl_18, tbl_19, tbl_20, tbl_21, tbl_22, tbl_23, tbl_24, tbl_25, tbl_26, tbl_27, tbl_28, tbl_29, tbl_30, tbl_31, W_top1, b_top1, W_top2, b_top2, W_top3 = _rec_inputs()

    def _L0_rec_setup():
        import jax, jax.numpy as jnp
        import numpy as np
        B, F, D = (256, 32, 64)
        LAYER_SIZE = (128, 128)

        def _cin_layer(h, x0, W, b):
            bsz, H, d = h.shape
            M = x0.shape[1]
            z = jnp.einsum('bhd,bmd->bhmd', h, x0).reshape(bsz, H * M, d)
            out = jnp.einsum('bcd,oc->bod', z, W) + b[None, :, None]
            return jax.nn.relu(out)
        key = jax.random.key(seed)
        k1, k2, k3 = jax.random.split(key, 3)
        inputs = jax.random.normal(k1, (B, F, D), dtype=jnp.float32)
        W0 = jax.random.normal(k2, (LAYER_SIZE[0], F * F), dtype=jnp.float32) * 0.03
        b0 = jnp.zeros((LAYER_SIZE[0],), dtype=jnp.float32)
        W1 = jax.random.normal(k3, (LAYER_SIZE[1], LAYER_SIZE[0] // 2 * F), dtype=jnp.float32) * 0.03
        b1 = jnp.zeros((LAYER_SIZE[1],), dtype=jnp.float32)
        return {'inputs': inputs, 'W0': W0, 'b0': b0, 'W1': W1, 'b1': b1}
    _L0_rec_all = _L0_rec_setup()
    _L0_rec_in = {k: v for k, v in _L0_rec_all.items() if k in ('W0', 'b0', 'W1', 'b1')}
    del _L0_rec_all
    return {'dense_ctx': dense_ctx, 'ids': ids, 'tbl_0': tbl_0, 'tbl_1': tbl_1, 'tbl_2': tbl_2, 'tbl_3': tbl_3, 'tbl_4': tbl_4, 'tbl_5': tbl_5, 'tbl_6': tbl_6, 'tbl_7': tbl_7, 'tbl_8': tbl_8, 'tbl_9': tbl_9, 'tbl_10': tbl_10, 'tbl_11': tbl_11, 'tbl_12': tbl_12, 'tbl_13': tbl_13, 'tbl_14': tbl_14, 'tbl_15': tbl_15, 'tbl_16': tbl_16, 'tbl_17': tbl_17, 'tbl_18': tbl_18, 'tbl_19': tbl_19, 'tbl_20': tbl_20, 'tbl_21': tbl_21, 'tbl_22': tbl_22, 'tbl_23': tbl_23, 'tbl_24': tbl_24, 'tbl_25': tbl_25, 'tbl_26': tbl_26, 'tbl_27': tbl_27, 'tbl_28': tbl_28, 'tbl_29': tbl_29, 'tbl_30': tbl_30, 'tbl_31': tbl_31, 'W_top1': W_top1, 'b_top1': b_top1, 'W_top2': W_top2, 'b_top2': b_top2, 'W_top3': W_top3, 'L0_rec_W0': _L0_rec_in['W0'], 'L0_rec_b0': _L0_rec_in['b0'], 'L0_rec_W1': _L0_rec_in['W1'], 'L0_rec_b1': _L0_rec_in['b1']}

def reference(dense_ctx, ids, tbl_0, tbl_1, tbl_2, tbl_3, tbl_4, tbl_5, tbl_6, tbl_7, tbl_8, tbl_9, tbl_10, tbl_11, tbl_12, tbl_13, tbl_14, tbl_15, tbl_16, tbl_17, tbl_18, tbl_19, tbl_20, tbl_21, tbl_22, tbl_23, tbl_24, tbl_25, tbl_26, tbl_27, tbl_28, tbl_29, tbl_30, tbl_31, W_top1, b_top1, W_top2, b_top2, W_top3, L0_rec_W0, L0_rec_b0, L0_rec_W1, L0_rec_b1):
    import jax
    import jax.numpy as jnp

    def _L0_rec_ref(inputs, W0, b0, W1, b1):
        import jax, jax.numpy as jnp
        import numpy as np
        B, F, D = (256, 32, 64)
        LAYER_SIZE = (128, 128)

        def _cin_layer(h, x0, W, b):
            bsz, H, d = h.shape
            M = x0.shape[1]
            z = jnp.einsum('bhd,bmd->bhmd', h, x0).reshape(bsz, H * M, d)
            out = jnp.einsum('bcd,oc->bod', z, W) + b[None, :, None]
            return jax.nn.relu(out)
        out0 = _cin_layer(inputs, inputs, W0, b0)
        half = LAYER_SIZE[0] // 2
        next_hidden = out0[:, :half, :]
        direct0 = out0[:, half:, :]
        direct1 = _cin_layer(next_hidden, inputs, W1, b1)
        result = jnp.concatenate([direct0, direct1], axis=1)
        return jnp.sum(result, axis=-1)
    e = jnp.stack([tbl_0[ids[:, 0]], tbl_1[ids[:, 1]], tbl_2[ids[:, 2]], tbl_3[ids[:, 3]], tbl_4[ids[:, 4]], tbl_5[ids[:, 5]], tbl_6[ids[:, 6]], tbl_7[ids[:, 7]], tbl_8[ids[:, 8]], tbl_9[ids[:, 9]], tbl_10[ids[:, 10]], tbl_11[ids[:, 11]], tbl_12[ids[:, 12]], tbl_13[ids[:, 13]], tbl_14[ids[:, 14]], tbl_15[ids[:, 15]], tbl_16[ids[:, 16]], tbl_17[ids[:, 17]], tbl_18[ids[:, 18]], tbl_19[ids[:, 19]], tbl_20[ids[:, 20]], tbl_21[ids[:, 21]], tbl_22[ids[:, 22]], tbl_23[ids[:, 23]], tbl_24[ids[:, 24]], tbl_25[ids[:, 25]], tbl_26[ids[:, 26]], tbl_27[ids[:, 27]], tbl_28[ids[:, 28]], tbl_29[ids[:, 29]], tbl_30[ids[:, 30]], tbl_31[ids[:, 31]]], axis=1)
    z = _L0_rec_ref(e, L0_rec_W0, L0_rec_b0, L0_rec_W1, L0_rec_b1)
    z = z.reshape(z.shape[0], -1)
    h = jnp.concatenate([z, dense_ctx], axis=1)
    h = jnp.maximum(h @ W_top1 + b_top1, 0.0)
    h = jnp.maximum(h @ W_top2 + b_top2, 0.0)
    y = h @ W_top3
    return y

_drawn_inputs = setup_inputs


def setup_inputs(seed=0):
    import zlib

    import numpy as np

    out = dict(_drawn_inputs(seed))
    spreads = {'b_top1': (0.0, 2.0),
     'b_top2': (0.0, 2.0),
     'L0_rec_b0': (0.0, 0.1),
     'L0_rec_b1': (0.0, 0.584)}
    factors = {'tbl_0': 8.0,
     'tbl_1': 8.0,
     'tbl_2': 8.0,
     'tbl_3': 8.0,
     'tbl_4': 8.0,
     'tbl_5': 8.0,
     'tbl_6': 8.0,
     'tbl_7': 8.0,
     'tbl_8': 8.0,
     'tbl_9': 8.0,
     'tbl_10': 8.0,
     'tbl_11': 8.0,
     'tbl_12': 8.0,
     'tbl_13': 8.0,
     'tbl_14': 8.0,
     'tbl_15': 8.0,
     'tbl_16': 8.0,
     'tbl_17': 8.0,
     'tbl_18': 8.0,
     'tbl_19': 8.0,
     'tbl_20': 8.0,
     'tbl_21': 8.0,
     'tbl_22': 8.0,
     'tbl_23': 8.0,
     'tbl_24': 8.0,
     'tbl_25': 8.0,
     'tbl_26': 8.0,
     'tbl_27': 8.0,
     'tbl_28': 8.0,
     'tbl_29': 8.0,
     'tbl_30': 8.0,
     'tbl_31': 8.0,
     'L0_rec_W0': 8.0,
     'L0_rec_W1': 7.734,
     'dense_ctx': 8.0}
    for name, (base, spread) in spreads.items():
        noise = np.random.default_rng([zlib.crc32(name.encode()), seed]).standard_normal(out[name].shape)
        drawn = base * np.exp(spread * noise) if base else spread * noise
        out[name] = jnp.asarray(drawn.astype(out[name].dtype))
    for name, factor in factors.items():
        out[name] = (out[name] * factor).astype(out[name].dtype)
    return out
```

```python
import numpy as np
import concourse.bass as bass
import concourse.mybir as mybir
from contextlib import ExitStack



def cin_tower_program(nc, ids, ident, w0_fwd, w0_rev, w1, b0, b1, dense, wt1a, wt1b, bt1, wt2, bt2,
                      wt3, tables, y):
    fp32 = mybir.dt.float32
    ALU = mybir.AluOpType
    ACT = mybir.ActivationFunctionType
    AX = mybir.AxisListType

    P = 128
    Q = 32
    F = len(tables)
    D = tables[0].shape[1]
    B = y.shape[0]
    G = B // P
    ND = 4
    N = ND * P
    BPG = D // ND
    T = G * BPG
    NR = F // 4
    RT = NR + 1
    CHUNKS = [(0, 2), (2, 4), (4, 6), (6, 8), (8, 9)]
    NC = len(CHUNKS)
    Z0 = NR // 2 + 1
    Z1 = 2 * NR
    ZH = Z1 // 2
    ZT = Z0 + Z1
    NZ = 7
    SL = 8 * F
    ES = F + 24
    HID = 64
    J1 = wt1a.shape[1] // P
    J2 = wt2.shape[2] // P
    GATHERED = 16 * F

    with ExitStack() as ctx:
        def sb(name, shape, dt=fp32):
            return ctx.enter_context(nc.sbuf_tensor(name, shape, dt))

        def sem(name):
            return ctx.enter_context(nc.semaphore(name))

        ids_sb = sb("ids_sb", [P, G * F], mybir.dt.int32)
        ident_sb = sb("ident_sb", [P, P])
        w0_sb = sb("w0_sb", [P, Z0, P])
        w0r_sb = sb("w0r_sb", [P, Z0 - 2, P])
        w1_sb = sb("w1_sb", [P, Z1, P])
        b0_sb = sb("b0_sb", [P, 1])
        b1_sb = sb("b1_sb", [P, 1])
        wt1a_sb = sb("wt1a_sb", [P, J1 * P])
        wt1b_sb = sb("wt1b_sb", [P, J1 * P])
        bt1_sb = sb("bt1_sb", [P, J1])
        wt2_sb = sb("wt2_sb", [P, J1, J2 * P])
        bt2_sb = sb("bt2_sb", [P, J2])
        wt3_sb = sb("wt3_sb", [P, J2])
        emb = sb("emb", [P, ES, 2, D])
        stage = sb("stage", [P, 2, ND, SL])
        feat = sb("feat", [P, 2, RT, N])
        prod = sb("prod", [P, NZ, N])
        hid = sb("hid", [P, 2, 2, N])
        rel0 = sb("rel0", [P, 2, N])
        rel1 = sb("rel1", [P, 2, N])
        acc0 = sb("acc0", [P, G * N])
        acc1 = sb("acc1", [P, G * N])
        top_a = sb("top_a", [P, B])
        top_b = sb("top_b", [P, B])
        h1 = sb("h1", [P, J1, B])
        h2 = sb("h2", [P, J2, B])
        y_sb = sb("y_sb", [1, B])

        turn = [ctx.enter_context(nc.psum_tensor(f"turn{i}", [P, 2 * N], fp32)) for i in range(2)]
        out0 = [ctx.enter_context(nc.psum_tensor(f"out0_{i}", [P, N], fp32)) for i in range(2)]
        out1 = [ctx.enter_context(nc.psum_tensor(f"out1_{i}", [P, N], fp32)) for i in range(2)]
        banks = [turn[0][:, 0:N], turn[0][:, N:2 * N], turn[1][:, 0:N], turn[1][:, N:2 * N],
                 out0[0][:, :], out0[1][:, :], out1[0][:, :], out1[1][:, :]]

        ids_loaded = sem("ids_loaded")
        gathered = sem("gathered")
        doubled = sem("doubled")
        ident_loaded = sem("ident_loaded")
        w0_loaded = sem("w0_loaded")
        w0_summed = sem("w0_summed")
        w1_loaded = sem("w1_loaded")
        bias_loaded = sem("bias_loaded")
        top_loaded = sem("top_loaded")
        acc_cleared = sem("acc_cleared")
        staged = sem("staged")
        turned = sem("turned")
        feat_ready = sem("feat_ready")
        prod_ready = sem("prod_ready")
        prod_used = sem("prod_used")
        hid_ready = sem("hid_ready")
        rel0_ready = sem("rel0_ready")
        rel1_ready = sem("rel1_ready")
        pooled0 = sem("pooled0")
        pooled1 = sem("pooled1")
        folded = sem("folded")
        top_sum = sem("top_sum")
        top_act = sem("top_act")
        stored = sem("stored")

        def wait(eng, semaphore, value):
            if not isinstance(value, int) or value > 0:
                eng.wait_ge(semaphore, value)

        def products_before(t):
            return Z0 + ZT * t

        def layer0_done(t):
            return products_before(t) - ZH if not (isinstance(t, int) and t == 0) else Z0

        def layer1_done(t):
            return products_before(t + 1) - (Z0 if is_last(t) else 0)

        def steps(eng, step):
            step(0, 0)
            step(1, 1)
            with eng.Fori(1, T // 2 - 1) as pair:
                step(pair * 2, 0)
                step(pair * 2 + 1, 1)
            step(T - 2, 0)
            step(T - 1, 1)

        def is_last(t):
            return isinstance(t, int) and t == T - 1

        block = ctx.enter_context(nc.Block())

        @block.sync
        def _(sp):
            sp.dma_start(ids_sb[:, :], ids).then_inc(ids_loaded, 16)
            sp.dma_start(ident_sb[:, :], ident).then_inc(ident_loaded, 16)
            sp.dma_start(w0_sb[:, :, :], w0_fwd).then_inc(w0_loaded, 16)
            sp.dma_start(w0r_sb[:, :, :], w0_rev).then_inc(w0_loaded, 16)
            sp.dma_start(b0_sb[:, :], b0).then_inc(bias_loaded, 16)
            sp.dma_start(b1_sb[:, :], b1).then_inc(bias_loaded, 16)
            sp.dma_start(w1_sb[:, :, :], w1).then_inc(w1_loaded, 16)
            sp.dma_start(top_a[0:HID, :], dense).then_inc(top_loaded, 16)
            sp.dma_start(wt1a_sb[:, :], wt1a).then_inc(top_loaded, 16)
            sp.dma_start(wt1b_sb[:, :], wt1b).then_inc(top_loaded, 16)
            sp.dma_start(bt1_sb[:, :], bt1).then_inc(top_loaded, 16)
            sp.dma_start(wt2_sb[:, :, :], wt2).then_inc(top_loaded, 16)
            sp.dma_start(bt2_sb[:, :], bt2).then_inc(top_loaded, 16)
            sp.dma_start(wt3_sb[:, :], wt3).then_inc(top_loaded, 16)
            sp.wait_ge(top_act, 2 * J1 + 2 * J2 + 2)
            sp.dma_start(y.rearrange("b a -> a b"), y_sb[:, :]).then_inc(stored, 16)
            sp.wait_ge(stored, 16)

        @block.gpsimd
        def _(pool):
            def gather(g, par):
                for f in range(F):
                    nc.gpsimd.indirect_dma_start(
                        emb[:, f, par, :], None, tables[f],
                        bass.IndirectOffsetOnAxis(ap=ids_sb[:, g * F + f:g * F + f + 1], axis=0)).then_inc(gathered, 16)
                pool.wait_ge(gathered, GATHERED * (g + 1))
                nc.gpsimd.tensor_copy(emb[:, F:ES, par, :], emb[:, 0:ES - F, par, :]).then_inc(doubled, 1)

            pool.wait_ge(ids_loaded, 16)
            gather(0, 0)
            nc.gpsimd.memset(acc0[:, :], 0.0).then_inc(acc_cleared, 1)
            nc.gpsimd.memset(acc1[:, :], 0.0).then_inc(acc_cleared, 1)
            gather(1, 1)
            for g in range(2, G):
                pool.wait_ge(staged, BPG * (g - 1))
                gather(g, g % 2)

        @block.scalar
        def _(act):
            def stage_block(t, par):
                wait(act, doubled, t // BPG + 1)
                wait(act, turned, NC * (t - 1))
                for turn8, lo in ((8, 0), (0, SL // 2)):
                    src = bass.AP(emb, (t & (2 * BPG - 1)) * ND,
                                  [[ES * 2 * D, P], [1, ND], [turn8 * 2 * D, 4], [2 * D, F]])
                    dst = stage[:, par, :, lo:lo + SL // 2].rearrange("p d (c f) -> p d c f", f=F)
                    last = nc.scalar.activation(dst, src, ACT.Copy)
                last.then_inc(staged, 1)

            def copy_chunk(t, par, c):
                lo, hi = CHUNKS[c]
                n = (NC * par + c) % 2
                wait(act, turned, NC * t + c + 1)
                nc.scalar.activation(feat[:, par, lo:hi, :],
                                     turn[n][:, 0:(hi - lo) * N].rearrange("p (r n) -> p r n", n=N),
                                     ACT.Copy).then_inc(feat_ready, 1)

            def relu0(t, par):
                wait(act, prod_used, layer0_done(t))
                for q in (0, 2):
                    last = nc.scalar.activation(hid[Q * q:Q * q + HID, par, 0, :], out0[par][0:HID, :],
                                                ACT.Relu, bias=b0_sb[0:HID, :])
                last.then_inc(hid_ready, 1)
                for q in range(4):
                    h = (q + 1) % 2
                    last = nc.scalar.activation(hid[Q * q:Q * q + Q, par, 1, :], out0[par][Q * h:Q * h + Q, :],
                                                ACT.Relu, bias=b0_sb[Q * h:Q * h + Q, :])
                last.then_inc(hid_ready, 1)
                wait(act, pooled0, t - 1)
                nc.scalar.activation(rel0[HID:P, par, :], out0[par][HID:P, :], ACT.Relu,
                                     bias=b0_sb[HID:P, :]).then_inc(rel0_ready, 1)

            def relu1(t, par):
                wait(act, prod_used, layer1_done(t))
                wait(act, pooled1, t - 1)
                nc.scalar.activation(rel1[:, par, :], out1[par][:, :], ACT.Relu,
                                     bias=b1_sb[:, :]).then_inc(rel1_ready, 1)

            stage_block(0, 0)
            stage_block(1, 1)
            for c in range(NC):
                copy_chunk(0, 0, c)
            act.wait_ge(bias_loaded, 32)
            relu0(0, 0)

            def step(t, par):
                if not is_last(t):
                    wait(act, prod_ready, products_before(t))
                    copy_chunk(t + 1, 1 - par, 0)
                    copy_chunk(t + 1, 1 - par, 1)
                if not (isinstance(t, int) and t == 0):
                    relu1(t - 1, 1 - par)
                if not is_last(t):
                    for c in range(2, NC):
                        copy_chunk(t + 1, 1 - par, c)
                    relu0(t + 1, 1 - par)
                if not (isinstance(t, int) and t >= T - 2):
                    stage_block(t + 2, par)

            steps(act, step)
            relu1(T - 1, 1)

            act.wait_ge(top_loaded, 16 * 7)
            for half in range(2):
                for j in range(J1):
                    act.wait_ge(top_sum, half * J1 + j + 1)
                    nc.scalar.activation(h1[:, j, half * N:half * N + N], banks[half * J1 + j], ACT.Relu,
                                         bias=bt1_sb[:, j:j + 1]).then_inc(top_act, 1)
            for half in range(2):
                for j in range(J2):
                    act.wait_ge(top_sum, 2 * J1 + half * J2 + j + 1)
                    nc.scalar.activation(h2[:, j, half * N:half * N + N], banks[half * J2 + j], ACT.Relu,
                                         bias=bt2_sb[:, j:j + 1]).then_inc(top_act, 1)
            for half in range(2):
                act.wait_ge(top_sum, 2 * J1 + 2 * J2 + half + 1)
                nc.scalar.activation(y_sb[:, half * N:half * N + N], banks[4 + half][0:1, :], ACT.Copy)\
                    .then_inc(top_act, 1)

        @block.vector
        def _(dve):
            def next_slot(n, slot):
                wait(dve, prod_used, n - NZ + 1)
                return prod[:, slot, :]

            def products0(t, par, n, slot):
                for k in range(Z0):
                    wait(dve, feat_ready, NC * t + (k + 1) // 2 + 1)
                    z = next_slot(n + k, (slot + k) % NZ)
                    nc.vector.tensor_tensor(z, feat[:, par, 0, :], feat[:, par, 1 + k, :],
                                            op=ALU.mult).then_inc(prod_ready, 1)

            def products1(t, par, way, n, slot):
                wait(dve, hid_ready, 2 * t + way + 1)
                if way == 0:
                    wait(dve, feat_ready, NC * (t + 1))
                for k in range(NR):
                    z = next_slot(n + k, (slot + k) % NZ)
                    nc.vector.tensor_tensor(z, hid[:, par, way, :], feat[:, par, 1 + k, :],
                                            op=ALU.mult).then_inc(prod_ready, 1)

            def pool0(t, par):
                wait(dve, rel0_ready, t + 1)
                wait(dve, pooled0, t)
                a = acc0[HID:P, bass.ds((t // BPG) * N, N)]
                nc.vector.tensor_tensor(a, a, rel0[HID:P, par, :], op=ALU.add).then_inc(pooled0, 1)

            def pool1(t, par):
                wait(dve, rel1_ready, t + 1)
                wait(dve, pooled1, t)
                a = acc1[:, bass.ds((t // BPG) * N, N)]
                nc.vector.tensor_tensor(a, a, rel1[:, par, :], op=ALU.add).then_inc(pooled1, 1)

            dve.wait_ge(w0_loaded, 32)
            nc.vector.tensor_tensor(w0_sb[:, 1:Z0 - 1, :], w0_sb[:, 1:Z0 - 1, :], w0r_sb[:, :, :], op=ALU.add)\
                .then_inc(w0_summed, 1)
            products0(0, 0, 0, 0)
            dve.wait_ge(acc_cleared, 2)

            def step(t, par):
                n = products_before(t)
                slot = (Z0 + ZT * par) % NZ
                products1(t, par, 0, n, slot)
                pool0(t, par)
                if not is_last(t):
                    products0(t + 1, 1 - par, n + ZH, (slot + ZH) % NZ)
                    n, slot = n + Z0, slot + Z0
                if not (isinstance(t, int) and t == 0):
                    pool1(t - 1, 1 - par)
                products1(t, par, 1, n + ZH, (slot + ZH) % NZ)

            steps(dve, step)
            pool1(T - 1, 1)

            dve.wait_ge(top_loaded, 16 * 7)
            dve.wait_ge(pooled0, T)
            dve.wait_ge(pooled1, T)
            HG = G // 2
            for half in range(2):
                cols = slice(half * HG * N, (half + 1) * HG * N)
                for acc, top, lo in ((acc0, top_a, HID), (acc1, top_b, 0)):
                    nc.vector.tensor_reduce(
                        top[lo:P, half * N:half * N + N].rearrange("p (g b) -> p g b", b=P),
                        acc[lo:P, cols].rearrange("p (g d b) -> p g b d", d=ND, b=P),
                        axis=AX.X, op=ALU.add).then_inc(folded, 1)

        @block.tensor
        def _(pe):
            def turn_chunk(t, par, c):
                lo, hi = CHUNKS[c]
                n = (NC * par + c) % 2
                if c == 0:
                    wait(pe, staged, t + 1)
                wait(pe, feat_ready, NC * t + c - 1)
                for r in range(lo, hi):
                    for d in range(ND):
                        slot = r - 1 if r else SL // 2
                        features = stage[:, par, d, slot:slot + P]
                        at = (r - lo) * N + d * P
                        last = nc.tensor.matmul(turn[n][:, at:at + P], features, ident_sb[:, :],
                                                start=True, stop=True, is_transpose=True)
                last.then_inc(turned, 1)

            def layer0(t, par, n, slot):
                wait(pe, rel0_ready, t - 1)
                for k in range(Z0):
                    wait(pe, prod_ready, n + k + 1)
                    last = nc.tensor.matmul(out0[par][:, :], w0_sb[:, k, :],
                                            prod[:, (slot + k) % NZ, :],
                                            start=(k == 0), stop=(k == Z0 - 1))
                    last.then_inc(prod_used, 1)

            def layer1(t, par, k, n, slot):
                if k == 0:
                    wait(pe, rel1_ready, t - 1)
                wait(pe, prod_ready, n + 1)
                nc.tensor.matmul(out1[par][:, :], w1_sb[:, k, :], prod[:, slot % NZ, :],
                                 start=(k == 0), stop=(k == Z1 - 1)).then_inc(prod_used, 1)

            pe.wait_ge(ident_loaded, 16)
            for c in range(NC):
                turn_chunk(0, 0, c)
            pe.wait_ge(w0_summed, 1)
            layer0(0, 0, 0, 0)
            pe.wait_ge(w1_loaded, 16)

            def step(t, par):
                n = products_before(t)
                slot = (Z0 + ZT * par) % NZ
                for k in range(ZH):
                    if k < NC and not is_last(t):
                        turn_chunk(t + 1, 1 - par, k)
                    layer1(t, par, k, n + k, slot + k)
                if not is_last(t):
                    layer0(t + 1, 1 - par, n + ZH, (slot + ZH) % NZ)
                    n, slot = n + Z0, slot + Z0
                for k in range(ZH, Z1):
                    layer1(t, par, k, n + k, slot + k)

            steps(pe, step)

            pe.wait_ge(top_loaded, 16 * 7)
            pe.wait_ge(rel1_ready, T)
            for half in range(2):
                cols = slice(half * N, half * N + N)
                pe.wait_ge(folded, 2 * half + 2)
                for j in range(J1):
                    bank = banks[half * J1 + j]
                    nc.tensor.matmul(bank, wt1a_sb[:, j * P:j * P + P], top_a[:, cols], start=True, stop=False)
                    nc.tensor.matmul(bank, wt1b_sb[:, j * P:j * P + P], top_b[:, cols], start=False, stop=True)\
                        .then_inc(top_sum, 1)
            for half in range(2):
                cols = slice(half * N, half * N + N)
                pe.wait_ge(top_act, (half + 1) * J1)
                for j in range(J2):
                    for i in range(J1):
                        last = nc.tensor.matmul(banks[half * J2 + j], wt2_sb[:, i, j * P:j * P + P], h1[:, i, cols],
                                                start=(i == 0), stop=(i == J1 - 1))
                    last.then_inc(top_sum, 1)
            for half in range(2):
                cols = slice(half * N, half * N + N)
                pe.wait_ge(top_act, 2 * J1 + (half + 1) * J2)
                for i in range(J2):
                    last = nc.tensor.matmul(banks[4 + half][0:1, :], wt3_sb[:, i:i + 1], h2[:, i, cols],
                                            start=(i == 0), stop=(i == J2 - 1))
                last.then_inc(top_sum, 1)


def kernel(**inputs):
    import concourse.bacc as _bacc
    from concourse.bass_utils import run_bass_kernel_spmd as _run

    P, F = 128, 32
    x = {k: np.asarray(v) for k, v in inputs.items()}
    B = x["ids"].shape[0]
    G = B // P
    f = np.arange(F)

    def partner(k, q):
        return (f + k + 8 * q + 8 * (f + k >= F)) % F

    w0 = x["L0_rec_W0"].reshape(P, F, F)
    fwd = np.zeros((P, 5, P), np.float32)
    rev = np.zeros((P, 3, P), np.float32)
    w1s = x["L0_rec_W1"].reshape(P, 2, F, F)
    w1 = np.zeros((P, 16, P), np.float32)
    for q in range(4):
        rows = slice(F * q, F * q + F)
        for k in range(8):
            if k < 5:
                fwd[rows, k, :] = w0[:, f, partner(k, q)].T
            if 0 < k < 4:
                rev[rows, k - 1, :] = w0[:, partner(k, q), f].T
            for way in range(2):
                w1[rows, way * 8 + k, :] = w1s[:, (q + way) % 2, f, partner(k, q)].T
    wt1 = x["W_top1"]
    nd = x["dense_ctx"].shape[1]
    wt1a = np.zeros((P, wt1.shape[1]), np.float32)
    wt1a[0:nd] = wt1[192:192 + nd]
    wt1a[64:128] = wt1[0:64]
    dense = np.zeros((64, B), np.float32)
    dense[0:nd] = x["dense_ctx"].T
    arrays = {
        "ids": x["ids"].reshape(G, P, F).transpose(1, 0, 2).reshape(P, G * F),
        "ident": np.eye(P, dtype=np.float32),
        "w0_fwd": fwd, "w0_rev": rev, "w1": w1,
        "b0": x["L0_rec_b0"].reshape(P, 1), "b1": x["L0_rec_b1"].reshape(P, 1),
        "dense": dense, "wt1a": wt1a, "wt1b": wt1[64:192],
        "bt1": x["b_top1"].reshape(4, P).T,
        "wt2": x["W_top2"].reshape(4, P, 256).transpose(1, 0, 2),
        "bt2": x["b_top2"].reshape(2, P).T,
        "wt3": x["W_top3"].reshape(2, P).T,
    }
    names = list(arrays)
    for i in range(F):
        arrays[f"tbl_{i}"] = x[f"tbl_{i}"]
    nc = _bacc.Bacc("TRN2", target_bir_lowering=False, num_devices=1)
    aps, feed = {}, {}
    for name, a in arrays.items():
        a = np.ascontiguousarray(a)
        feed[f"in_{name}_dram"] = a
        aps[name] = nc.dram_tensor(f"in_{name}_dram", a.shape, mybir.dt.from_np(a.dtype), kind="ExternalInput").ap()
    y = nc.dram_tensor("out_0_dram", (B, 1), mybir.dt.float32, kind="ExternalOutput").ap()
    cin_tower_program(nc, *[aps[n] for n in names], [aps[f"tbl_{i}"] for i in range(F)], y)
    r = _run(nc, [feed], core_ids=[0])
    return r.results[0]["out_0_dram"]
```

```python
import numpy as np
import concourse.bass as bass
import concourse.mybir as mybir
from contextlib import ExitStack



def cin_tower_program(nc, ids, ident, w0_fwd, w0_rev, w0_far, w1, b0, b1, dense, wt1a, wt1b, bt1, wt2, bt2,
                      wt3, tables, y):
    fp32 = mybir.dt.float32
    fp32r = mybir.dt.float32r
    ALU = mybir.AluOpType
    ACT = mybir.ActivationFunctionType
    AX = mybir.AxisListType

    P = 128
    Q = 32
    F = len(tables)
    D = tables[0].shape[1]
    B = y.shape[0]
    G = B // P
    ND = 4
    N = ND * P
    BPG = D // ND
    T = G * BPG
    NR = F // 4
    RT = NR + 1
    LOADS = [(0, 3), (3, 7), (7, RT)]
    Z0 = NR // 2
    Z1 = 2 * NR
    ZH = Z1 // 2
    WAY_MADE = [("split", 0), ("whole", 2), ("whole", 4), ("low", 0), ("whole", 6)]
    WAY_TAKEN = [2, 4, 6, 0]
    SPLIT = [k for kind, k in WAY_MADE if kind == "split"]
    NSH = len(SPLIT)
    NSP = 2 * NSH
    NH = ZH // 2 - NSH
    ZT = Z0 // 2 + 2 * NH
    NZ = 4
    NS = 2
    HID = 64
    J1 = wt1a.shape[1] // P
    J2 = wt2.shape[2] // P
    FEAT_LOADED = 16 * 4
    GATHERED = 16 * F

    with ExitStack() as ctx:
        def sb(name, shape, dt=fp32):
            return ctx.enter_context(nc.sbuf_tensor(name, shape, dt))

        def sem(name):
            return ctx.enter_context(nc.semaphore(name))

        ids_sb = sb("ids_sb", [P, G * F], mybir.dt.int32)
        ident_sb = sb("ident_sb", [P, P])
        w0_sb = sb("w0_sb", [P, Z0, P])
        w0r_sb = sb("w0r_sb", [P, Z0, P])
        w0m_sb = sb("w0m_sb", [3 * Q, P])
        w0m_high = sb("w0m_high", [3 * Q, P], fp32r)
        w0m_stack = sb("w0m_stack", [3 * Q, P], fp32r)
        w1_sb = sb("w1_sb", [P, Z1, P])
        b0_sb = sb("b0_sb", [P, 1])
        b1_sb = sb("b1_sb", [P, 1])
        wt1a_sb = sb("wt1a_sb", [P, J1 * P])
        wt1b_sb = sb("wt1b_sb", [P, J1 * P])
        bt1_sb = sb("bt1_sb", [P, J1])
        wt2_sb = sb("wt2_sb", [P, J1, J2 * P])
        bt2_sb = sb("bt2_sb", [P, J2])
        wt3_sb = sb("wt3_sb", [P, J2])
        emb = sb("emb", [P, F, 2, D])
        stage = sb("stage", [P, 2, F, ND])
        turned_x = sb("turned_x", [P, 2, P])
        feat = sb("feat", [P, 2, RT, N])
        prod = sb("prod", [P, NZ, 2, N])
        full = sb("full", [P, NS, 2, N])
        high = sb("high", [P, NS, 2, N], fp32r)
        low = sb("low", [P, NS, 2, N], fp32r)
        far = sb("far", [Q, 2, N])
        far_stack = sb("far_stack", [3 * Q, 2, N], fp32r)
        w1_high = sb("w1_high", [P, NSP, 2, P], fp32r)
        w1_low = sb("w1_low", [P, NSP, 2, P], fp32r)
        hid = sb("hid", [P, 2, 2, N])
        rel0 = sb("rel0", [P, 2, N])
        rel1 = sb("rel1", [P, 2, N])
        acc0 = sb("acc0", [P, G * N])
        acc1 = sb("acc1", [P, G * N])
        emb_flat = emb[:, :, :, :].rearrange("p f a d -> p (f a d)")
        top_a = emb_flat[:, 0:B]
        top_b = emb_flat[:, B:2 * B]
        feat_flat = feat[:, :, :, :].rearrange("p a r n -> p (a r n)")
        h1 = feat_flat[:, 0:J1 * B].rearrange("p (j b) -> p j b", b=B)
        h2 = feat_flat[:, J1 * B:(J1 + J2) * B].rearrange("p (j b) -> p j b", b=B)
        y_sb = feat_flat[0:1, (J1 + J2) * B:(J1 + J2 + 1) * B]

        turn_x = ctx.enter_context(nc.psum_tensor("turn_x", [P, N], fp32))
        out0 = [ctx.enter_context(nc.psum_tensor(f"out0_{i}", [P, N], fp32)) for i in range(2)]
        out1 = [ctx.enter_context(nc.psum_tensor(f"out1_{i}", [P, N], fp32)) for i in range(2)]
        spare = [ctx.enter_context(nc.psum_tensor(f"tower_{i}", [P, N], fp32)) for i in range(3)]
        banks = [x[:, :] for x in spare + [turn_x] + out0 + out1]
        scratch = nc.dram_tensor("features_by_row", (2 * 2 * F * N,), fp32)

        ids_loaded = sem("ids_loaded")
        gathered = sem("gathered")
        ident_loaded = sem("ident_loaded")
        w0_loaded = sem("w0_loaded")
        w0_summed = sem("w0_summed")
        w0m_rounded = sem("w0m_rounded")
        w0m_split = sem("w0m_split")
        w1_loaded = sem("w1_loaded")
        bias_loaded = sem("bias_loaded")
        top_loaded = sem("top_loaded")
        acc_cleared = sem("acc_cleared")
        staged = sem("staged")
        x_turned = sem("x_turned")
        x_copied = sem("x_copied")
        x_stored = sem("x_stored")
        feat_loaded = [[sem(f"feat_loaded_{i}_{par}") for par in range(2)] for i in range(len(LOADS))]
        prod_ready = sem("prod_ready")
        prod_used = sem("prod_used")
        full_ready = sem("full_ready")
        high_ready = sem("high_ready")
        low_ready = sem("low_ready")
        split_used = sem("split_used")
        far_ready = sem("far_ready")
        far_rounded = sem("far_rounded")
        far_split = sem("far_split")
        far_used = sem("far_used")
        w1_rounded = sem("w1_rounded")
        w1_split = sem("w1_split")
        hid_ready = sem("hid_ready")
        rel0_ready = sem("rel0_ready")
        rel1_ready = sem("rel1_ready")
        pooled0 = sem("pooled0")
        pooled1 = sem("pooled1")
        folded = sem("folded")
        top_sum = sem("top_sum")
        top_act = sem("top_act")
        stored = sem("stored")

        def wait(eng, semaphore, value):
            if not isinstance(value, int) or value > 0:
                eng.wait_ge(semaphore, value)

        def products_before(t):
            return Z0 // 2 + ZT * t

        def wait_features(dve, part, t, par):
            each = FEAT_LOADED * (2 if part == 0 else 1)
            wait(dve, feat_loaded[part][par], each // 2 * (t + 2 - par))

        def steps(eng, step):
            step(0, 0)
            step(1, 1)
            with eng.Fori(1, T // 2 - 2) as pair:
                step(pair * 2, 0)
                step(pair * 2 + 1, 1)
            for t in range(T - 4, T):
                step(t, t % 2)

        def is_last(t):
            return isinstance(t, int) and t == T - 1

        block = ctx.enter_context(nc.Block())

        @block.sync
        def _(sp):
            sp.dma_start(ids_sb[:, :], ids).then_inc(ids_loaded, 16)
            sp.dma_start(ident_sb[:, :], ident).then_inc(ident_loaded, 16)
            sp.dma_start(w0_sb[:, :, :], w0_fwd).then_inc(w0_loaded, 16)
            sp.dma_start(w0r_sb[:, :, :], w0_rev).then_inc(w0_loaded, 16)
            sp.dma_start(w0m_sb[:, :], w0_far).then_inc(w0_loaded, 16)
            sp.dma_start(b0_sb[:, :], b0).then_inc(bias_loaded, 16)
            sp.dma_start(b1_sb[:, :], b1).then_inc(bias_loaded, 16)
            sp.dma_start(w1_sb[:, :, :], w1).then_inc(w1_loaded, 16)
            sp.dma_start(wt1a_sb[:, :], wt1a).then_inc(top_loaded, 16)
            sp.dma_start(wt1b_sb[:, :], wt1b).then_inc(top_loaded, 16)
            sp.dma_start(bt1_sb[:, :], bt1).then_inc(top_loaded, 16)
            sp.dma_start(wt2_sb[:, :, :], wt2).then_inc(top_loaded, 16)
            sp.dma_start(bt2_sb[:, :], bt2).then_inc(top_loaded, 16)
            sp.dma_start(wt3_sb[:, :], wt3).then_inc(top_loaded, 16)
            def store_x(t, par, made=0):
                wait(sp, x_copied, t + 1)
                for copy in range(2):
                    if copy:
                        wait(sp, full_ready, made)
                    dst = bass.AP(scratch, (2 * par + copy) * F * N, [[P, P], [1, P]])
                    sp.dma_start(dst, turned_x[:, par, :]).then_inc(x_stored, 16)

            def load_features(t, par, part):
                lo, hi = LOADS[part]
                for q in range(4):
                    rows = slice(Q * q, Q * q + Q)
                    if lo == 0:
                        sp.dma_start(feat[rows, par, 0, :], bass.AP(scratch, 2 * par * F * N, [[N, Q], [1, N]]))\
                            .then_inc(feat_loaded[part][par], 16)
                    first = max(lo, 1)
                    src = bass.AP(scratch, (2 * par * F + 4 * (first - 1) + q) * N,
                                  [[N, Q], [4 * N, hi - first], [1, N]])
                    sp.dma_start(feat[rows, par, first:hi, :], src).then_inc(feat_loaded[part][par], 16)

            store_x(0, 0)
            store_x(1, 1)
            sp.wait_ge(x_stored, 64)
            for part in range(len(LOADS)):
                load_features(0, 0, part)

            def step(t, par):
                if not is_last(t):
                    wait(sp, x_stored, 32 * (t + 2))
                    if isinstance(t, int) and t == T - 2:
                        sp.wait_ge(full_ready, NSP * t)
                    load_features(t + 1, 1 - par, 0)
                    wait(sp, prod_ready, products_before(t) - 1)
                    load_features(t + 1, 1 - par, 1)
                    wait(sp, prod_ready, products_before(t))
                    load_features(t + 1, 1 - par, 2)
                if not (isinstance(t, int) and t >= T - 2):
                    store_x(t + 2, par, NSP * (t + 1))

            steps(sp, step)
            sp.wait_ge(staged, T)
            sp.dma_start(top_a[0:HID, :], dense).then_inc(top_loaded, 16)
            sp.wait_ge(top_act, 2 * J1 + 2 * J2 + 2)
            sp.dma_start(y.rearrange("b a -> a b"), y_sb).then_inc(stored, 16)
            sp.wait_ge(stored, 16)

        @block.gpsimd
        def _(pool):
            pool.wait_ge(ids_loaded, 16)
            for g in range(G):
                if g >= 2:
                    pool.wait_ge(staged, BPG * (g - 1))
                for f in range(F):
                    nc.gpsimd.indirect_dma_start(
                        emb[:, f, g % 2, :], None, tables[f],
                        bass.IndirectOffsetOnAxis(ap=ids_sb[:, g * F + f:g * F + f + 1], axis=0))\
                        .then_inc(gathered, 16)
                if g == 0:
                    nc.gpsimd.memset(acc0[:, :], 0.0).then_inc(acc_cleared, 1)
                    nc.gpsimd.memset(acc1[:, :], 0.0).then_inc(acc_cleared, 1)
                pool.wait_ge(gathered, GATHERED * (g + 1))

        @block.scalar
        def _(act):
            def stage_block(t, par):
                wait(act, gathered, GATHERED * (t // BPG + 1))
                wait(act, x_turned, t - 1)
                src = bass.AP(emb, (t & (2 * BPG - 1)) * ND, [[F * 2 * D, P], [2 * D, F], [1, ND]])
                nc.scalar.activation(stage[:, par, :, :], src, ACT.Copy).then_inc(staged, 1)

            def copy_x(t, par):
                wait(act, x_turned, t + 1)
                wait(act, x_stored, 32 * (t - 1))
                nc.scalar.activation(turned_x[:, par, :], turn_x[:, 0:P], ACT.Copy).then_inc(x_copied, 1)

            def round_pair(t, way, i):
                m = NSP * t + NSH * way + i
                at = (NSH * way + i) % NS
                wait(act, full_ready, m + 1)
                wait(act, split_used, m - NS + 1)
                nc.scalar.activation(high[:, at, :, :], full[:, at, :, :], ACT.Copy).then_inc(high_ready, 1)

            def round_far(t, par):
                wait(act, far_ready, t + 1)
                wait(act, far_used, t - 1)
                for q in (0, 2):
                    nc.scalar.activation(far_stack[Q * q:Q * q + Q, par, :], far[:, par, :], ACT.Copy)\
                        .then_inc(far_rounded, 1)

            def relu0(t, par):
                wait(act, prod_ready, products_before(t - 1))
                wait(act, far_used, t + 1)
                for q in (0, 2):
                    last = nc.scalar.activation(hid[Q * q:Q * q + HID, par, 0, :], out0[par][0:HID, :],
                                                ACT.Relu, bias=b0_sb[0:HID, :])
                last.then_inc(hid_ready, 1)
                for q in range(4):
                    h = (q + 1) % 2
                    last = nc.scalar.activation(hid[Q * q:Q * q + Q, par, 1, :], out0[par][Q * h:Q * h + Q, :],
                                                ACT.Relu, bias=b0_sb[Q * h:Q * h + Q, :])
                last.then_inc(hid_ready, 1)
                wait(act, pooled0, t - 1)
                nc.scalar.activation(rel0[HID:P, par, :], out0[par][HID:P, :], ACT.Relu,
                                     bias=b0_sb[HID:P, :]).then_inc(rel0_ready, 1)

            def relu1(t, par):
                wait(act, split_used, NSP * (t + 1))
                wait(act, pooled1, t - 1)
                nc.scalar.activation(rel1[:, par, :], out1[par][:, :], ACT.Relu,
                                     bias=b1_sb[:, :]).then_inc(rel1_ready, 1)

            stage_block(0, 0)
            stage_block(1, 1)
            copy_x(0, 0)
            copy_x(1, 1)
            stage_block(2, 0)
            act.wait_ge(w0_loaded, 48)
            nc.scalar.activation(w0m_high[:, :], w0m_sb[:, :], ACT.Copy).then_inc(w0m_rounded, 1)
            nc.scalar.activation(w0m_stack[0:2 * Q, :], w0m_sb[0:2 * Q, :], ACT.Copy).then_inc(w0m_rounded, 1)
            round_far(0, 0)
            act.wait_ge(w1_loaded, 16)
            for way in range(2):
                for i, k in enumerate(SPLIT):
                    k += way * ZH
                    nc.scalar.activation(w1_high[:, way * NSH + i, :, :], w1_sb[:, k:k + 2, :], ACT.Copy)\
                        .then_inc(w1_rounded, 1)
            act.wait_ge(bias_loaded, 32)
            relu0(0, 0)
            round_pair(0, 0, 0)

            def step(t, par):
                more = not is_last(t)
                if not (isinstance(t, int) and t == 0):
                    relu1(t - 1, 1 - par)
                if not (isinstance(t, int) and t >= T - 2):
                    copy_x(t + 2, par)
                if more:
                    round_far(t + 1, 1 - par)
                for i in range(NSH):
                    round_pair(t, 1, i)
                if more:
                    relu0(t + 1, 1 - par)
                if more:
                    round_pair(t + 1, 0, 0)
                if not (isinstance(t, int) and t >= T - 3):
                    stage_block(t + 3, 1 - par)

            steps(act, step)
            relu1(T - 1, 1)

            act.wait_ge(top_loaded, 16 * 7)
            for half in range(2):
                for j in range(J1):
                    act.wait_ge(top_sum, half * J1 + j + 1)
                    nc.scalar.activation(h1[:, j, half * N:half * N + N], banks[half * J1 + j], ACT.Relu,
                                         bias=bt1_sb[:, j:j + 1]).then_inc(top_act, 1)
            for half in range(2):
                for j in range(J2):
                    act.wait_ge(top_sum, 2 * J1 + half * J2 + j + 1)
                    nc.scalar.activation(h2[:, j, half * N:half * N + N], banks[half * J2 + j], ACT.Relu,
                                         bias=bt2_sb[:, j:j + 1]).then_inc(top_act, 1)
            for half in range(2):
                act.wait_ge(top_sum, 2 * J1 + 2 * J2 + half + 1)
                nc.scalar.activation(y_sb[:, half * N:half * N + N], banks[4 + half][0:1, :], ACT.Copy)\
                    .then_inc(top_act, 1)

        @block.vector
        def _(dve):
            def next_pair(n, at):
                wait(dve, prod_used, n - NZ + 1)
                return prod[:, at % NZ, :, :]

            def twice(tile):
                return bass.AP(tile.tensor, tile.offset, [tile.ap[0], [0, 2], [1, N]])

            def products0(t, par, n, at):
                features = feat[:, par, 0, :]
                wait_features(dve, 0, t, par)
                for k in range(0, Z0, 2):
                    if k == 2:
                        wait_features(dve, 1, t, par)
                    z = next_pair(n + k // 2, at + k // 2)
                    nc.vector.tensor_tensor(z, twice(features), feat[:, par, 1 + k:3 + k, :], op=ALU.mult)\
                        .then_inc(prod_ready, 1)
                wait(dve, far_split, t - 1)
                nc.vector.tensor_tensor(far[:, par, :], feat[0:Q, par, 0, :], feat[0:Q, par, 1 + Z0, :],
                                        op=ALU.mult).then_inc(far_ready, 1)

            def split_far(t, par):
                wait(dve, far_rounded, 2 * (t + 1))
                wait(dve, far_used, t - 1)
                nc.vector.tensor_tensor(far_stack[Q:2 * Q, par, :], far[:, par, :],
                                        far_stack[0:Q, par, :].bitcast(fp32), op=ALU.subtract)\
                    .then_inc(far_split, 1)

            def products1(t, par, way, n, at):
                wait(dve, hid_ready, 2 * t + way + 1)
                if way == 0:
                    wait_features(dve, 2, t, par)
                hidden = hid[:, par, way, :]
                for kind, k in WAY_MADE:
                    partners = feat[:, par, 1 + k:3 + k, :]
                    if kind == "whole":
                        z = next_pair(n, at)
                        nc.vector.tensor_tensor(z, twice(hidden), partners, op=ALU.mult).then_inc(prod_ready, 1)
                        n, at = n + 1, at + 1
                        continue
                    i = SPLIT.index(k)
                    m = NSP * t + NSH * way + i
                    slot = (NSH * way + i) % NS
                    if kind == "split":
                        wait(dve, low_ready, m - NS + 1)
                        nc.vector.tensor_tensor(full[:, slot, :, :], twice(hidden), partners, op=ALU.mult)\
                            .then_inc(full_ready, 1)
                    else:
                        wait(dve, high_ready, m + 1)
                        wait(dve, split_used, m - NS + 1)
                        nc.vector.tensor_tensor(low[:, slot, :, :], full[:, slot, :, :],
                                                high[:, slot, :, :].bitcast(fp32), op=ALU.subtract)\
                            .then_inc(low_ready, 1)

            def pool0(t, par):
                wait(dve, rel0_ready, t + 1)
                wait(dve, pooled0, t)
                a = acc0[HID:P, bass.ds((t // BPG) * N, N)]
                nc.vector.tensor_tensor(a, a, rel0[HID:P, par, :], op=ALU.add).then_inc(pooled0, 1)

            def pool1(t, par):
                wait(dve, rel1_ready, t + 1)
                wait(dve, pooled1, t)
                a = acc1[:, bass.ds((t // BPG) * N, N)]
                nc.vector.tensor_tensor(a, a, rel1[:, par, :], op=ALU.add).then_inc(pooled1, 1)

            dve.wait_ge(w0_loaded, 48)
            nc.vector.tensor_tensor(w0_sb[:, :, :], w0_sb[:, :, :], w0r_sb[:, :, :], op=ALU.add)\
                .then_inc(w0_summed, 1)
            products0(0, 0, 0, 0)
            dve.wait_ge(w0m_rounded, 2)
            nc.vector.tensor_tensor(w0m_stack[2 * Q:3 * Q, :], w0m_sb[2 * Q:3 * Q, :],
                                    w0m_high[2 * Q:3 * Q, :].bitcast(fp32), op=ALU.subtract)\
                .then_inc(w0m_split, 1)
            split_far(0, 0)
            for way in range(2):
                for i, k in enumerate(SPLIT):
                    j = way * NSH + i
                    dve.wait_ge(w1_rounded, j + 1)
                    k += way * ZH
                    nc.vector.tensor_tensor(w1_low[:, j, :, :], w1_sb[:, k:k + 2, :],
                                            w1_high[:, j, :, :].bitcast(fp32), op=ALU.subtract)\
                        .then_inc(w1_split, 1)
            dve.wait_ge(acc_cleared, 2)

            def step(t, par):
                n = products_before(t)
                at = products_before(par)
                products1(t, par, 0, n, at)
                pool0(t, par)
                n, at = n + NH, at + NH
                if not is_last(t):
                    products0(t + 1, 1 - par, n, at)
                    n, at = n + Z0 // 2, at + Z0 // 2
                if not (isinstance(t, int) and t == 0):
                    pool1(t - 1, 1 - par)
                if not is_last(t):
                    split_far(t + 1, 1 - par)
                products1(t, par, 1, n, at)

            steps(dve, step)
            pool1(T - 1, 1)

            dve.wait_ge(top_loaded, 16 * 7)
            dve.wait_ge(pooled0, T)
            dve.wait_ge(pooled1, T)
            HG = G // 2
            for half in range(2):
                cols = slice(half * HG * N, (half + 1) * HG * N)
                for acc, top, lo in ((acc0, top_a, HID), (acc1, top_b, 0)):
                    nc.vector.tensor_reduce(
                        top[lo:P, half * N:half * N + N].rearrange("p (g b) -> p g b", b=P),
                        acc[lo:P, cols].rearrange("p (g d b) -> p g b d", d=ND, b=P),
                        axis=AX.X, op=ALU.add).then_inc(folded, 1)

        @block.tensor
        def _(pe):
            def turn_features(t, par):
                wait(pe, staged, t + 1)
                wait(pe, x_copied, t)
                nc.tensor.matmul(turn_x[:, 0:P], stage[:, par, :, :].rearrange("p f d -> p (f d)"), ident_sb[:, :],
                                 start=True, stop=True, is_transpose=True).then_inc(x_turned, 1)

            def layer0(t, par, n, at):
                wait(pe, rel0_ready, t - 1)
                for k in range(Z0):
                    wait(pe, prod_ready, n + k // 2 + 1)
                    last = nc.tensor.matmul(out0[par][:, :], w0_sb[:, k, :], prod[:, (at + k // 2) % NZ, k % 2, :],
                                            start=(k == 0), stop=False)
                    if k % 2:
                        last.then_inc(prod_used, 1)
                wait(pe, far_rounded, 2 * (t + 1))
                wait(pe, far_split, t + 1)
                nc.tensor.matmul(out0[par][:, :], w0m_stack[:, :], far_stack[:, par, :], start=False, stop=True)\
                    .then_inc(far_used, 1)

            def layer1(t, par, way, n, at):
                if way == 0:
                    wait(pe, rel1_ready, t - 1)
                for turn_no, k in enumerate(WAY_TAKEN):
                    for half in range(2):
                        c = 2 * turn_no + half
                        start = way == 0 and c == 0
                        stop = way == 1 and c == ZH - 1
                        if k not in SPLIT:
                            wait(pe, prod_ready, n + 1)
                            last = nc.tensor.matmul(out1[par][:, :], w1_sb[:, way * ZH + k + half, :],
                                                    prod[:, at % NZ, half, :], start=start, stop=stop)
                            if half:
                                last.then_inc(prod_used, 1)
                                n, at = n + 1, at + 1
                            continue
                        j = NSH * way + SPLIT.index(k)
                        m, slot = NSP * t + j, j % NS
                        wait(pe, high_ready, m + 1)
                        nc.tensor.matmul(out1[par][:, :], w1_high[:, j, half, :], high[:, slot, half, :],
                                         start=start, stop=False)
                        nc.tensor.matmul(out1[par][:, :], w1_low[:, j, half, :], high[:, slot, half, :],
                                         start=False, stop=False)
                        wait(pe, low_ready, m + 1)
                        last = nc.tensor.matmul(out1[par][:, :], w1_high[:, j, half, :], low[:, slot, half, :],
                                                start=False, stop=stop)
                        if half:
                            last.then_inc(split_used, 1)

            pe.wait_ge(ident_loaded, 16)
            turn_features(0, 0)
            turn_features(1, 1)
            pe.wait_ge(w0_summed, 1)
            pe.wait_ge(w0m_split, 1)
            layer0(0, 0, 0, 0)
            pe.wait_ge(w1_loaded, 16)
            pe.wait_ge(w1_split, NSP)

            def step(t, par):
                n = products_before(t)
                at = products_before(par)
                if not (isinstance(t, int) and t >= T - 2):
                    turn_features(t + 2, par)
                layer1(t, par, 0, n, at)
                n, at = n + NH, at + NH
                if not is_last(t):
                    layer0(t + 1, 1 - par, n, at)
                    n, at = n + Z0 // 2, at + Z0 // 2
                layer1(t, par, 1, n, at)

            steps(pe, step)

            pe.wait_ge(top_loaded, 16 * 7)
            pe.wait_ge(rel1_ready, T)
            for half in range(2):
                cols = slice(half * N, half * N + N)
                pe.wait_ge(folded, 2 * half + 2)
                for j in range(J1):
                    bank = banks[half * J1 + j]
                    nc.tensor.matmul(bank, wt1a_sb[:, j * P:j * P + P], top_a[:, cols], start=True, stop=False)
                    nc.tensor.matmul(bank, wt1b_sb[:, j * P:j * P + P], top_b[:, cols], start=False, stop=True)\
                        .then_inc(top_sum, 1)
            for half in range(2):
                cols = slice(half * N, half * N + N)
                pe.wait_ge(top_act, (half + 1) * J1)
                for j in range(J2):
                    for i in range(J1):
                        last = nc.tensor.matmul(banks[half * J2 + j], wt2_sb[:, i, j * P:j * P + P], h1[:, i, cols],
                                                start=(i == 0), stop=(i == J1 - 1))
                    last.then_inc(top_sum, 1)
            for half in range(2):
                cols = slice(half * N, half * N + N)
                pe.wait_ge(top_act, 2 * J1 + (half + 1) * J2)
                for i in range(J2):
                    last = nc.tensor.matmul(banks[4 + half][0:1, :], wt3_sb[:, i:i + 1], h2[:, i, cols],
                                            start=(i == 0), stop=(i == J2 - 1))
                last.then_inc(top_sum, 1)


def kernel(**inputs):
    import concourse.bacc as _bacc
    from concourse.bass_utils import run_bass_kernel_spmd as _run

    P, F = 128, 32
    x = {k: np.asarray(v) for k, v in inputs.items()}
    B = x["ids"].shape[0]
    G = B // P
    f = np.arange(F)

    def partner(k, q):
        return (f + 4 * k + q) % F

    w0 = x["L0_rec_W0"].reshape(P, F, F)
    fwd = np.zeros((P, 4, P), np.float32)
    rev = np.zeros((P, 4, P), np.float32)
    far = np.concatenate([w0[:, f, partner(4, 0)].T] * 3)
    w1s = x["L0_rec_W1"].reshape(P, 2, F, F)
    w1 = np.zeros((P, 16, P), np.float32)
    for q in range(4):
        rows = slice(F * q, F * q + F)
        for k in range(8):
            if k < 4:
                fwd[rows, k, :] = w0[:, f, partner(k, q)].T
            if k < 4 and k + q > 0:
                rev[rows, k, :] = w0[:, partner(k, q), f].T
            for way in range(2):
                w1[rows, way * 8 + k, :] = w1s[:, (q + way) % 2, f, partner(k, q)].T
    wt1 = x["W_top1"]
    nd = x["dense_ctx"].shape[1]
    wt1a = np.zeros((P, wt1.shape[1]), np.float32)
    wt1a[0:nd] = wt1[192:192 + nd]
    wt1a[64:128] = wt1[0:64]
    dense = np.zeros((64, B), np.float32)
    dense[0:nd] = x["dense_ctx"].T
    arrays = {
        "ids": x["ids"].reshape(G, P, F).transpose(1, 0, 2).reshape(P, G * F),
        "ident": np.eye(P, dtype=np.float32),
        "w0_fwd": fwd, "w0_rev": rev, "w0_far": far, "w1": w1,
        "b0": x["L0_rec_b0"].reshape(P, 1), "b1": x["L0_rec_b1"].reshape(P, 1),
        "dense": dense, "wt1a": wt1a, "wt1b": wt1[64:192],
        "bt1": x["b_top1"].reshape(4, P).T,
        "wt2": x["W_top2"].reshape(4, P, 256).transpose(1, 0, 2),
        "bt2": x["b_top2"].reshape(2, P).T,
        "wt3": x["W_top3"].reshape(2, P).T,
    }
    names = list(arrays)
    for i in range(F):
        arrays[f"tbl_{i}"] = x[f"tbl_{i}"]
    nc = _bacc.Bacc("TRN2", target_bir_lowering=False, num_devices=1)
    aps, feed = {}, {}
    for name, a in arrays.items():
        a = np.ascontiguousarray(a)
        feed[f"in_{name}_dram"] = a
        aps[name] = nc.dram_tensor(f"in_{name}_dram", a.shape, mybir.dt.from_np(a.dtype), kind="ExternalInput").ap()
    y = nc.dram_tensor("out_0_dram", (B, 1), mybir.dt.float32, kind="ExternalOutput").ap()
    cin_tower_program(nc, *[aps[n] for n in names], [aps[f"tbl_{i}"] for i in range(F)], y)
    r = _run(nc, [feed], core_ids=[0])
    return r.results[0]["out_0_dram"]
```

```python
import numpy as np
import concourse.bass as bass
import concourse.mybir as mybir
from contextlib import ExitStack



def cin_tower_program(nc, ids, ident, w0_fwd, w0_rev, w0_far, w1, b0, b1, dense, wt1a, wt1b, bt1, wt2, bt2,
                      wt3, tables, y):
    fp32 = mybir.dt.float32
    fp32r = mybir.dt.float32r
    ALU = mybir.AluOpType
    ACT = mybir.ActivationFunctionType
    AX = mybir.AxisListType

    P = 128
    Q = 32
    F = len(tables)
    D = tables[0].shape[1]
    B = y.shape[0]
    G = B // P
    ND = 4
    N = ND * P
    BPG = D // ND
    T = G * BPG
    NR = F // 4
    RT = NR + 1
    LOADS = [(0, 3), (3, 7), (7, RT)]
    Z0 = NR // 2
    Z1 = 2 * NR
    ZH = Z1 // 2
    MADE = [[("split", 0), ("whole", 2), ("split", 4), ("split", 6)],
            [("split", 0), ("split", 2), ("whole", 4), ("split", 6)]]
    TAKEN = [[2, 0, 4, 6], [0, 4, 2, 6]]
    SPLIT = [(way, k) for way in range(2) for kind, k in MADE[way] if kind == "split"]
    NSP = len(SPLIT)
    EARLY = 1
    BY_DVE = 2
    NS0 = sum(way == 0 for way, _ in SPLIT)
    NH = [sum(kind == "whole" for kind, _ in MADE[way]) for way in range(2)]
    ZT = Z0 // 2 + sum(NH)
    NZ = 4
    NF = 4
    HID = 64
    J1 = wt1a.shape[1] // P
    J2 = wt2.shape[2] // P
    FEAT_LOADED = [16 * 6, 16 * 4, 16 * 4]
    PER_STEP = 3
    GATHERED = 16 * F

    with ExitStack() as ctx:
        def sb(name, shape, dt=fp32):
            return ctx.enter_context(nc.sbuf_tensor(name, shape, dt))

        def sem(name):
            return ctx.enter_context(nc.semaphore(name))

        ids_sb = sb("ids_sb", [P, G * F], mybir.dt.int32)
        ids_now = sb("ids_now", [P, 2, F], mybir.dt.int32)
        ident_sb = sb("ident_sb", [P, P])
        w0_sb = sb("w0_sb", [P, Z0, P])
        w0m_sb = sb("w0m_sb", [3 * Q, P])
        w0m_high = sb("w0m_high", [3 * Q, P], fp32r)
        w0m_stack = sb("w0m_stack", [3 * Q, P], fp32r)
        w1_sb = sb("w1_sb", [P, Z1, P])
        b0_sb = sb("b0_sb", [P, 1])
        b1_sb = sb("b1_sb", [P, 1])
        bt1_sb = sb("bt1_sb", [P, J1])
        bt2_sb = sb("bt2_sb", [P, J2])
        wt3_sb = sb("wt3_sb", [P, J2])
        emb = sb("emb", [P, F, 2, D])
        stage = sb("stage", [P, 2, F, ND])
        turned_x = sb("turned_x", [P, 2, P])
        feat = sb("feat", [P, 2, RT, N])
        prod = sb("prod", [P, NZ, 2, N])
        full = sb("full", [P, NF, 2, N])
        w0r_sb = full[:, 0, 0, :].rearrange("p (k m) -> p k m", m=P)
        high = sb("high", [P, NSP, 2, N], fp32r)
        low = sb("low", [P, NSP, 2, N], fp32r)
        far = sb("far", [Q, 2, N])
        far_stack = sb("far_stack", [3 * Q, 2, N], fp32r)
        w1_high = sb("w1_high", [P, NSP, 2, P], fp32r)
        w1_low = sb("w1_low", [P, NSP, 2, P], fp32r)
        rel0 = sb("rel0", [P, N])
        rel1 = sb("rel1", [P, 2, N])
        acc0 = sb("acc0", [P, G * N])
        acc1 = sb("acc1", [P, G * N])
        sums0 = sb("sums0", [P, N])
        emb_flat = emb[:, :, :, :].rearrange("p f a d -> p (f a d)")
        top_a = emb_flat[:, 0:B]
        top_b = emb_flat[:, B:2 * B]
        wt1a_sb = emb_flat[:, 2 * B:2 * B + J1 * P]
        wt1b_sb = emb_flat[:, 2 * B + J1 * P:2 * B + 2 * J1 * P]
        wt2_sb = emb_flat[:, 2 * B + 2 * J1 * P:2 * B + (2 + J2) * J1 * P].rearrange("p (i j) -> p i j", j=J2 * P)
        feat_flat = feat[:, :, :, :].rearrange("p a r n -> p (a r n)")
        h1 = feat_flat[:, 0:J1 * B].rearrange("p (j b) -> p j b", b=B)
        h2 = feat_flat[:, J1 * B:(J1 + J2) * B].rearrange("p (j b) -> p j b", b=B)
        y_sb = feat_flat[0:1, (J1 + J2) * B:(J1 + J2 + 1) * B]

        h1_high = high[:, :, :, :].rearrange("p s t n -> p (s t) n")
        h1_low = low[:, :, :, :].rearrange("p s t n -> p (s t) n")
        wt2_high = w1_high[:, :, :, :].rearrange("p s t m -> p (s t m)")[:, 0:J1 * J2 * P]
        wt2_low = w1_low[:, :, :, :].rearrange("p s t m -> p (s t m)")[:, 0:J1 * J2 * P]
        wt2_flat = wt2_sb.rearrange("p i j -> p (i j)")

        turn_x = ctx.enter_context(nc.psum_tensor("turn_x", [P, N], fp32))
        out0 = ctx.enter_context(nc.psum_tensor("out0", [P, N], fp32))
        out1 = [ctx.enter_context(nc.psum_tensor(f"out1_{i}", [P, N], fp32)) for i in range(2)]
        hid = [[ctx.enter_context(nc.psum_tensor(f"hid_{par}_{way}", [P, N], fp32)) for way in range(2)]
               for par in range(2)]
        banks = [x[:, :] for x in (*hid[0], turn_x, out0, out1[0], *hid[1], out1[1])]
        scratch = nc.dram_tensor("features_by_row", (2 * 2 * F * N,), fp32)

        ids_loaded = sem("ids_loaded")
        gathered = sem("gathered")
        ident_loaded = sem("ident_loaded")
        w0_loaded = sem("w0_loaded")
        w0_summed = sem("w0_summed")
        w0m_rounded = sem("w0m_rounded")
        w0m_split = sem("w0m_split")
        w1_loaded = sem("w1_loaded")
        bias_loaded = sem("bias_loaded")
        top_loaded = sem("top_loaded")
        acc_cleared = sem("acc_cleared")
        staged = sem("staged")
        x_turned = sem("x_turned")
        x_copied = sem("x_copied")
        x_stored = sem("x_stored")
        feat_loaded = [[sem(f"feat_loaded_{i}_{par}") for par in range(2)] for i in range(len(LOADS))]
        prod_ready = sem("prod_ready")
        prod_used = sem("prod_used")
        ids_picked = sem("ids_picked")
        full_ready = sem("full_ready")
        high_ready = sem("high_ready")
        low_by_pool = sem("low_by_pool")
        low_by_dve = sem("low_by_dve")
        split_used = sem("split_used")
        far_ready = sem("far_ready")
        far_rounded = sem("far_rounded")
        far_split = sem("far_split")
        far_used = sem("far_used")
        w1_rounded = sem("w1_rounded")
        w1_split = sem("w1_split")
        hid_ready = sem("hid_ready")
        rel0_ready = sem("rel0_ready")
        rel1_ready = sem("rel1_ready")
        pooled0 = sem("pooled0")
        pooled1 = sem("pooled1")
        summed0 = sem("summed0")
        folded0 = sem("folded0")
        folded1 = sem("folded1")
        top_sum = sem("top_sum")
        top_act = sem("top_act")
        wt2_rounded = sem("wt2_rounded")
        h1_rounded = sem("h1_rounded")
        wt2_split = sem("wt2_split")
        h1_split = sem("h1_split")
        stored = sem("stored")

        def wait(eng, semaphore, value):
            if not isinstance(value, int) or value > 0:
                eng.wait_ge(semaphore, value)

        def products_before(t):
            return Z0 // 2 + ZT * t

        def wait_low(eng, m):
            t, j = m
            if j == BY_DVE:
                wait(eng, low_by_dve, t + 1)
            else:
                wait(eng, low_by_pool, (NSP - 1) * t + (j if j < BY_DVE else j - 1) + 1)

        def wait_features(dve, part, t, par):
            wait(dve, feat_loaded[part][par], FEAT_LOADED[part] // 2 * (t + 2 - par))

        def steps(eng, step):
            step(0, 0)
            step(1, 1)
            with eng.Fori(1, T // 2 - 2) as pair:
                step(pair * 2, 0)
                step(pair * 2 + 1, 1)
            for t in range(T - 4, T):
                step(t, t % 2)

        def is_last(t):
            return isinstance(t, int) and t == T - 1

        block = ctx.enter_context(nc.Block())

        @block.sync
        def _(sp):
            sp.dma_start(ids_sb[:, :], ids).then_inc(ids_loaded, 16)
            sp.dma_start(ident_sb[:, :], ident).then_inc(ident_loaded, 16)
            sp.dma_start(w0_sb[:, :, :], w0_fwd).then_inc(w0_loaded, 16)
            sp.dma_start(w0r_sb, w0_rev).then_inc(w0_loaded, 16)
            sp.dma_start(w0m_sb[:, :], w0_far).then_inc(w0_loaded, 16)
            sp.dma_start(b0_sb[:, :], b0).then_inc(bias_loaded, 16)
            sp.dma_start(b1_sb[:, :], b1).then_inc(bias_loaded, 16)
            sp.dma_start(w1_sb[:, :, :], w1).then_inc(w1_loaded, 16)
            sp.dma_start(bt1_sb[:, :], bt1).then_inc(top_loaded, 16)
            sp.dma_start(bt2_sb[:, :], bt2).then_inc(top_loaded, 16)
            sp.dma_start(wt3_sb[:, :], wt3).then_inc(top_loaded, 16)
            def store_x(t, par, made=0):
                wait(sp, x_copied, t + 1)
                for copy in range(2):
                    if copy:
                        wait(sp, full_ready, made)
                    dst = bass.AP(scratch, (2 * par + copy) * F * N, [[P, P], [1, P]])
                    sp.dma_start(dst, turned_x[:, par, :]).then_inc(x_stored, 16)

            def load_features(t, par, part):
                lo, hi = LOADS[part]
                if lo == 0:
                    for q in (0, 2):
                        sp.dma_start(feat[Q * q:Q * q + 2 * Q, par, 0, :],
                                     bass.AP(scratch, 2 * par * F * N, [[N, 2 * Q], [1, N]]))\
                            .then_inc(feat_loaded[part][par], 16)
                first = max(lo, 1)
                for q in range(4):
                    rows = slice(Q * q, Q * q + Q)
                    src = bass.AP(scratch, (2 * par * F + 4 * (first - 1) + q) * N,
                                  [[N, Q], [4 * N, hi - first], [1, N]])
                    sp.dma_start(feat[rows, par, first:hi, :], src).then_inc(feat_loaded[part][par], 16)

            store_x(0, 0)
            sp.wait_ge(x_stored, 32)
            for part in range(len(LOADS)):
                load_features(0, 0, part)
            store_x(1, 1)

            def step(t, par):
                if not is_last(t):
                    wait(sp, x_stored, 32 * (t + 2))
                    if isinstance(t, int) and t == T - 2:
                        sp.wait_ge(full_ready, NSP * t - 2)
                    load_features(t + 1, 1 - par, 0)
                    wait(sp, prod_ready, products_before(t))
                    load_features(t + 1, 1 - par, 1)
                    wait(sp, full_ready, NSP * t)
                    load_features(t + 1, 1 - par, 2)
                if not (isinstance(t, int) and t >= T - 2):
                    store_x(t + 2, par, NSP * (t + 1) - 2)

            steps(sp, step)
            sp.wait_ge(staged, T)
            sp.dma_start(top_a[0:HID, :], dense).then_inc(top_loaded, 16)
            sp.dma_start(wt1a_sb, wt1a).then_inc(top_loaded, 16)
            sp.dma_start(wt1b_sb, wt1b).then_inc(top_loaded, 16)
            sp.dma_start(wt2_sb, wt2).then_inc(top_loaded, 16)
            sp.wait_ge(top_act, 2 * J1 + 2 * J2 + 2)
            sp.dma_start(y.rearrange("b a -> a b"), y_sb).then_inc(stored, 16)
            sp.wait_ge(stored, 16)

        @block.gpsimd
        def _(pool):
            def low_parts(t, par, way):
                for j, (w, _) in enumerate(SPLIT):
                    if w == way and j != BY_DVE:
                        at = (NSP * par + j) % NF
                        wait(pool, high_ready, NSP * t + j + 1)
                        nc.gpsimd.tensor_tensor(low[:, j, :, :], full[:, at, :, :],
                                                high[:, j, :, :].bitcast(fp32), op=ALU.subtract)\
                            .then_inc(low_by_pool, 1)

            def gather(f, par, ids_of_f):
                nc.gpsimd.indirect_dma_start(emb[:, f, par, :], None, tables[f],
                                             bass.IndirectOffsetOnAxis(ap=ids_of_f, axis=0))\
                    .then_inc(gathered, 16)

            def group(g, par, more):
                if more:
                    nc.gpsimd.tensor_copy(ids_now[:, 1 - par, :], ids_sb[:, bass.ds((g + 1) * F, F)])\
                        .then_inc(ids_picked, 1)
                f = 0
                for c in range(BPG):
                    t = g * BPG + c
                    if more and c == 0:
                        wait(pool, ids_picked, g + 1)
                    low_parts(t, c % 2, 0)
                    for _ in range(PER_STEP):
                        if more and f < F:
                            gather(f, 1 - par, ids_now[:, 1 - par, f:f + 1])
                            f += 1
                    low_parts(t, c % 2, 1)

            pool.wait_ge(ids_loaded, 16)
            for f in range(F):
                gather(f, 0, ids_sb[:, f:f + 1])
            nc.gpsimd.memset(acc0[:, :], 0.0).then_inc(acc_cleared, 1)
            nc.gpsimd.memset(acc1[:, :], 0.0).then_inc(acc_cleared, 1)
            with pool.Fori(0, G // 2 - 1) as pair:
                group(pair * 2, 0, True)
                group(pair * 2 + 1, 1, True)
            group(G - 2, 0, True)
            group(G - 1, 1, False)

        @block.scalar
        def _(act):
            def stage_block(t, par):
                wait(act, gathered, GATHERED * (t // BPG + 1))
                wait(act, x_turned, t - 1)
                src = bass.AP(emb, (t & (2 * BPG - 1)) * ND, [[F * 2 * D, P], [2 * D, F], [1, ND]])
                nc.scalar.activation(stage[:, par, :, :], src, ACT.Copy).then_inc(staged, 1)

            def copy_x(t, par):
                wait(act, x_turned, t + 1)
                wait(act, x_stored, 32 * (t - 1))
                wait(act, feat_loaded[-1][par], FEAT_LOADED[-1] // 2 * (t - par))
                nc.scalar.activation(turned_x[:, par, :], turn_x[:, 0:P], ACT.Copy).then_inc(x_copied, 1)

            def round_pair(t, par, j):
                wait(act, full_ready, NSP * t + j + 1)
                wait(act, split_used, NSP * (t - 1) + j + 1)
                nc.scalar.activation(high[:, j, :, :], full[:, (NSP * par + j) % NF, :, :], ACT.Copy)\
                    .then_inc(high_ready, 1)

            def round_far(t, par):
                wait(act, far_ready, t + 1)
                wait(act, far_used, t - 1)
                for q in (0, 2):
                    nc.scalar.activation(far_stack[Q * q:Q * q + Q, par, :], far[:, par, :], ACT.Copy)\
                        .then_inc(far_rounded, 1)

            def relu0(t, par):
                wait(act, far_used, t + 1)
                for q in (0, 2):
                    last = nc.scalar.activation(hid[par][0][Q * q:Q * q + HID, :], out0[0:HID, :],
                                                ACT.Relu, bias=b0_sb[0:HID, :])
                last.then_inc(hid_ready, 1)

            def relu0_direct(t, par):
                if par == 0:
                    wait(act, pooled0, t // 2)
                nc.scalar.activation(rel0[HID * par:HID * par + HID, :], out0[HID:P, :], ACT.Relu,
                                     bias=b0_sb[HID:P, :])\
                    .then_inc(rel0_ready, 1)

            def relu0_other_way(t, par):
                for q in range(4):
                    h = (q + 1) % 2
                    last = nc.scalar.activation(hid[par][1][Q * q:Q * q + Q, :], out0[Q * h:Q * h + Q, :],
                                                ACT.Relu, bias=b0_sb[Q * h:Q * h + Q, :])
                last.then_inc(hid_ready, 1)

            def relu1(t, par):
                wait(act, split_used, NSP * (t + 1))
                wait(act, pooled1, t - 1)
                nc.scalar.activation(rel1[:, par, :], out1[par][:, :], ACT.Relu,
                                     bias=b1_sb[:, :]).then_inc(rel1_ready, 1)

            act.wait_ge(w0_loaded, 48)
            nc.scalar.activation(w0m_high[:, :], w0m_sb[:, :], ACT.Copy).then_inc(w0m_rounded, 1)
            nc.scalar.activation(w0m_stack[0:2 * Q, :], w0m_sb[0:2 * Q, :], ACT.Copy).then_inc(w0m_rounded, 1)
            act.wait_ge(w1_loaded, 16)
            for j, (way, k) in enumerate(SPLIT):
                k += way * ZH
                nc.scalar.activation(w1_high[:, j, :, :], w1_sb[:, k:k + 2, :], ACT.Copy)\
                    .then_inc(w1_rounded, 1)
            stage_block(0, 0)
            stage_block(1, 1)
            copy_x(0, 0)
            copy_x(1, 1)
            stage_block(2, 0)
            round_far(0, 0)
            act.wait_ge(bias_loaded, 32)
            relu0(0, 0)
            relu0_direct(0, 0)
            round_pair(0, 0, 0)
            relu0_other_way(0, 0)
            for j in range(1, NS0):
                round_pair(0, 0, j)

            def step(t, par):
                more = not is_last(t)
                if not (isinstance(t, int) and t == 0):
                    relu1(t - 1, 1 - par)
                if not (isinstance(t, int) and t >= T - 2):
                    copy_x(t + 2, par)
                if not (isinstance(t, int) and t >= T - 3):
                    stage_block(t + 3, 1 - par)
                for j in range(NS0, NS0 + EARLY):
                    round_pair(t, par, j)
                if more:
                    round_far(t + 1, 1 - par)
                for j in range(NS0 + EARLY, NSP - 1):
                    round_pair(t, par, j)
                if more:
                    relu0(t + 1, 1 - par)
                round_pair(t, par, NSP - 1)
                if more:
                    relu0_direct(t + 1, 1 - par)
                    round_pair(t + 1, 1 - par, 0)
                    relu0_other_way(t + 1, 1 - par)
                    for j in range(1, NS0):
                        round_pair(t + 1, 1 - par, j)

            steps(act, step)
            relu1(T - 1, 1)

            act.wait_ge(top_loaded, 16 * 7)
            act.wait_ge(split_used, NSP * T)
            nc.scalar.activation(wt2_high, wt2_flat, ACT.Copy).then_inc(wt2_rounded, 1)
            for half in range(2):
                for j in range(J1):
                    act.wait_ge(top_sum, half * J1 + j + 1)
                    nc.scalar.activation(h1[:, j, half * N:half * N + N], banks[half * J1 + j], ACT.Relu,
                                         bias=bt1_sb[:, j:j + 1]).then_inc(top_act, 1)
                    act.wait_ge(top_act, half * J1 + j + 1)
                    nc.scalar.activation(h1_high[:, half * J1 + j, :], h1[:, j, half * N:half * N + N], ACT.Copy)\
                        .then_inc(h1_rounded, 1)
            for half in range(2):
                for j in range(J2):
                    act.wait_ge(top_sum, 2 * J1 + half * J2 + j + 1)
                    nc.scalar.activation(h2[:, j, half * N:half * N + N], banks[half * J2 + j], ACT.Relu,
                                         bias=bt2_sb[:, j:j + 1]).then_inc(top_act, 1)
            for half in range(2):
                act.wait_ge(top_sum, 2 * J1 + 2 * J2 + half + 1)
                nc.scalar.activation(y_sb[:, half * N:half * N + N], banks[4 + half][0:1, :], ACT.Copy)\
                    .then_inc(top_act, 1)

        @block.vector
        def _(dve):
            def next_pair(n, at):
                wait(dve, prod_used, n - NZ + 1)
                return prod[:, at % NZ, :, :]

            def twice(tile):
                return bass.AP(tile.tensor, tile.offset, [tile.ap[0], [0, 2], [1, N]])

            def products0(t, par, pair, n, at):
                wait_features(dve, pair, t, par)
                z = next_pair(n, at)
                nc.vector.tensor_tensor(z, twice(feat[:, par, 0, :]), feat[:, par, 1 + 2 * pair:3 + 2 * pair, :],
                                        op=ALU.mult).then_inc(prod_ready, 1)

            def far_product(t, par):
                wait_features(dve, 1, t, par)
                wait(dve, far_split, t - 1)
                nc.vector.tensor_tensor(far[:, par, :], feat[0:Q, par, 0, :], feat[0:Q, par, 1 + Z0, :],
                                        op=ALU.mult).then_inc(far_ready, 1)

            def split_far(t, par):
                wait(dve, far_rounded, 2 * (t + 1))
                wait(dve, far_used, t - 1)
                nc.vector.tensor_tensor(far_stack[Q:2 * Q, par, :], far[:, par, :],
                                        far_stack[0:Q, par, :].bitcast(fp32), op=ALU.subtract)\
                    .then_inc(far_split, 1)

            def products1(t, par, way, pairs, n, at):
                wait(dve, hid_ready, 2 * t + way + 1)
                if way == 0:
                    wait_features(dve, 2, t, par)
                hidden = hid[par][way][:, :]
                for kind, k in pairs:
                    partners = feat[:, par, 1 + k:3 + k, :]
                    if kind == "whole":
                        z = next_pair(n, at)
                        nc.vector.tensor_tensor(z, twice(hidden), partners, op=ALU.mult).then_inc(prod_ready, 1)
                    else:
                        j = SPLIT.index((way, k))
                        wait_low(dve, (t, j - NF) if j >= NF else (t - 1, j - NF + NSP))
                        nc.vector.tensor_tensor(full[:, (NSP * par + j) % NF, :, :], twice(hidden), partners,
                                                op=ALU.mult).then_inc(full_ready, 1)

            def low_part(t, par):
                wait(dve, high_ready, NSP * t + BY_DVE + 1)
                nc.vector.tensor_tensor(low[:, BY_DVE, :, :], full[:, (NSP * par + BY_DVE) % NF, :, :],
                                        high[:, BY_DVE, :, :].bitcast(fp32), op=ALU.subtract)\
                    .then_inc(low_by_dve, 1)

            def pool0(t):
                wait(dve, rel0_ready, t + 1)
                wait(dve, pooled0, t // 2)
                a = acc0[:, bass.ds((t // BPG) * N, N)]
                nc.vector.tensor_tensor(a, a, rel0[:, :], op=ALU.add).then_inc(pooled0, 1)

            def pool1(t, par):
                wait(dve, rel1_ready, t + 1)
                wait(dve, pooled1, t)
                a = acc1[:, bass.ds((t // BPG) * N, N)]
                nc.vector.tensor_tensor(a, a, rel1[:, par, :], op=ALU.add).then_inc(pooled1, 1)

            def over_dimensions(acc, half):
                cols = slice(half * (G // 2) * N, (half + 1) * (G // 2) * N)
                return acc[:, cols].rearrange("p (g d b) -> p g b d", d=ND, b=P)

            def fold0(half):
                dve.wait_ge(pooled0, T // 2)
                dve.wait_ge(folded0, half)
                nc.vector.tensor_reduce(sums0[:, :].rearrange("p (g b) -> p g b", b=P),
                                        over_dimensions(acc0, half), axis=AX.X, op=ALU.add)\
                    .then_inc(summed0, 1)
                top = top_a[HID:P, half * N:half * N + N]
                dve.wait_ge(summed0, 2 * half + 1)
                nc.vector.tensor_copy(top, sums0[0:HID, :]).then_inc(summed0, 1)
                dve.wait_ge(summed0, 2 * half + 2)
                nc.vector.tensor_tensor(top, top, sums0[HID:P, :], op=ALU.add).then_inc(folded0, 1)

            def fold1(half):
                dve.wait_ge(pooled1, T - 1 + half)
                nc.vector.tensor_reduce(top_b[:, half * N:half * N + N].rearrange("p (g b) -> p g b", b=P),
                                        over_dimensions(acc1, half), axis=AX.X, op=ALU.add)\
                    .then_inc(folded1, 1)

            dve.wait_ge(w0_loaded, 48)
            nc.vector.tensor_tensor(w0_sb[:, :, :], w0_sb[:, :, :], w0r_sb, op=ALU.add)\
                .then_inc(w0_summed, 1)
            dve.wait_ge(w0m_rounded, 2)
            nc.vector.tensor_tensor(w0m_stack[2 * Q:3 * Q, :], w0m_sb[2 * Q:3 * Q, :],
                                    w0m_high[2 * Q:3 * Q, :].bitcast(fp32), op=ALU.subtract)\
                .then_inc(w0m_split, 1)
            for j, (way, k) in enumerate(SPLIT):
                dve.wait_ge(w1_rounded, j + 1)
                k += way * ZH
                nc.vector.tensor_tensor(w1_low[:, j, :, :], w1_sb[:, k:k + 2, :],
                                        w1_high[:, j, :, :].bitcast(fp32), op=ALU.subtract)\
                    .then_inc(w1_split, 1)
            products0(0, 0, 0, 0, 0)
            products0(0, 0, 1, 1, 1)
            far_product(0, 0)
            split_far(0, 0)
            dve.wait_ge(acc_cleared, 2)

            def step(t, par):
                n = products_before(t)
                at = products_before(par)
                products1(t, par, 0, MADE[0], n, at)
                n, at = n + NH[0], at + NH[0]
                if par == 1:
                    pool0(t)
                if not is_last(t):
                    products0(t + 1, 1 - par, 0, n, at)
                products1(t, par, 1, MADE[1][:EARLY], n, at)
                if not is_last(t):
                    products0(t + 1, 1 - par, 1, n + 1, at + 1)
                    n, at = n + Z0 // 2, at + Z0 // 2
                low_part(t, par)
                if not is_last(t):
                    far_product(t + 1, 1 - par)
                if not (isinstance(t, int) and t == 0):
                    pool1(t - 1, 1 - par)
                products1(t, par, 1, MADE[1][EARLY:EARLY + 1], n, at)
                if not is_last(t):
                    split_far(t + 1, 1 - par)
                products1(t, par, 1, MADE[1][EARLY + 1:], n, at)

            steps(dve, step)
            dve.wait_ge(top_loaded, 16 * 7)
            fold1(0)
            fold0(0)
            pool1(T - 1, 1)
            fold1(1)
            fold0(1)
            dve.wait_ge(wt2_rounded, 1)
            nc.vector.tensor_tensor(wt2_low, wt2_flat, wt2_high.bitcast(fp32), op=ALU.subtract)\
                .then_inc(wt2_split, 1)
            for half in range(2):
                for j in range(J1):
                    dve.wait_ge(h1_rounded, half * J1 + j + 1)
                    nc.vector.tensor_tensor(h1_low[:, half * J1 + j, :], h1[:, j, half * N:half * N + N],
                                            h1_high[:, half * J1 + j, :].bitcast(fp32), op=ALU.subtract)\
                        .then_inc(h1_split, 1)

        @block.tensor
        def _(pe):
            def turn_features(t, par):
                wait(pe, staged, t + 1)
                wait(pe, x_copied, t)
                nc.tensor.matmul(turn_x[:, 0:P], stage[:, par, :, :].rearrange("p f d -> p (f d)"), ident_sb[:, :],
                                 start=True, stop=True, is_transpose=True).then_inc(x_turned, 1)

            def layer0(t, par, n, at):
                wait(pe, hid_ready, 2 * t)
                for k in range(Z0):
                    wait(pe, prod_ready, n + k // 2 + 1)
                    last = nc.tensor.matmul(out0[:, :], w0_sb[:, k, :], prod[:, (at + k // 2) % NZ, k % 2, :],
                                            start=(k == 0), stop=False)
                    if k % 2:
                        last.then_inc(prod_used, 1)
                wait(pe, far_rounded, 2 * (t + 1))
                wait(pe, far_split, t + 1)
                nc.tensor.matmul(out0[:, :], w0m_stack[:, :], far_stack[:, par, :], start=False, stop=True)\
                    .then_inc(far_used, 1)

            def layer1(t, par, way, pairs, n, at):
                if way == 0 and pairs[0] == TAKEN[0][0]:
                    wait(pe, rel1_ready, t - 1)
                for k in pairs:
                    start = way == 0 and k == TAKEN[0][0]
                    stop = way == 1 and k == TAKEN[1][-1]
                    if (way, k) not in SPLIT:
                        wait(pe, prod_ready, n + 1)
                        for half in range(2):
                            last = nc.tensor.matmul(out1[par][:, :], w1_sb[:, way * ZH + k + half, :],
                                                    prod[:, at % NZ, half, :], start=start and half == 0,
                                                    stop=stop and half == 1)
                        last.then_inc(prod_used, 1)
                        n, at = n + 1, at + 1
                        continue
                    j = SPLIT.index((way, k))
                    wait(pe, high_ready, NSP * t + j + 1)
                    for half in range(2):
                        nc.tensor.matmul(out1[par][:, :], w1_high[:, j, half, :], high[:, j, half, :],
                                         start=start and half == 0, stop=False)
                        nc.tensor.matmul(out1[par][:, :], w1_low[:, j, half, :], high[:, j, half, :],
                                         start=False, stop=False)
                    wait_low(pe, (t, j))
                    for half in range(2):
                        last = nc.tensor.matmul(out1[par][:, :], w1_high[:, j, half, :], low[:, j, half, :],
                                                start=False, stop=stop and half == 1)
                    last.then_inc(split_used, 1)

            pe.wait_ge(ident_loaded, 16)
            turn_features(0, 0)
            turn_features(1, 1)
            pe.wait_ge(w0_summed, 1)
            pe.wait_ge(w0m_split, 1)
            layer0(0, 0, 0, 0)
            pe.wait_ge(w1_loaded, 16)
            pe.wait_ge(w1_split, NSP)

            def step(t, par):
                n = products_before(t)
                at = products_before(par)
                if not (isinstance(t, int) and t >= T - 2):
                    turn_features(t + 2, par)
                layer1(t, par, 0, TAKEN[0][:-1], n, at)
                n, at = n + NH[0], at + NH[0]
                if not is_last(t):
                    layer0(t + 1, 1 - par, n, at)
                    n, at = n + Z0 // 2, at + Z0 // 2
                layer1(t, par, 0, TAKEN[0][-1:], n, at)
                layer1(t, par, 1, TAKEN[1], n, at)

            steps(pe, step)

            pe.wait_ge(top_loaded, 16 * 7)
            for half in range(2):
                cols = slice(half * N, half * N + N)
                pe.wait_ge(rel1_ready, T - 1 + half)
                pe.wait_ge(hid_ready, 2 * T)
                pe.wait_ge(folded1, half + 1)
                for j in range(J1):
                    nc.tensor.matmul(banks[half * J1 + j], wt1b_sb[:, j * P:j * P + P], top_b[:, cols],
                                     start=True, stop=False)
                pe.wait_ge(folded0, half + 1)
                for j in range(J1):
                    nc.tensor.matmul(banks[half * J1 + j], wt1a_sb[:, j * P:j * P + P], top_a[:, cols],
                                     start=False, stop=True).then_inc(top_sum, 1)
            for half in range(2):
                pe.wait_ge(wt2_split, 1)
                pe.wait_ge(h1_split, (half + 1) * J1)
                for j in range(J2):
                    for i in range(J1):
                        weights = slice((i * J2 + j) * P, (i * J2 + j + 1) * P)
                        part = half * J1 + i
                        nc.tensor.matmul(banks[half * J2 + j], wt2_high[:, weights], h1_high[:, part, :],
                                         start=(i == 0), stop=False)
                        nc.tensor.matmul(banks[half * J2 + j], wt2_low[:, weights], h1_high[:, part, :],
                                         start=False, stop=False)
                        last = nc.tensor.matmul(banks[half * J2 + j], wt2_high[:, weights], h1_low[:, part, :],
                                                start=False, stop=(i == J1 - 1))
                    last.then_inc(top_sum, 1)
            for half in range(2):
                cols = slice(half * N, half * N + N)
                pe.wait_ge(top_act, 2 * J1 + (half + 1) * J2)
                for i in range(J2):
                    last = nc.tensor.matmul(banks[4 + half][0:1, :], wt3_sb[:, i:i + 1], h2[:, i, cols],
                                            start=(i == 0), stop=(i == J2 - 1))
                last.then_inc(top_sum, 1)


def kernel(**inputs):
    import concourse.bacc as _bacc
    from concourse.bass_utils import run_bass_kernel_spmd as _run

    P, F = 128, 32
    x = {k: np.asarray(v) for k, v in inputs.items()}
    B = x["ids"].shape[0]
    G = B // P
    f = np.arange(F)

    def partner(k, q):
        return (f + 4 * k + q) % F

    w0 = x["L0_rec_W0"].reshape(P, F, F)
    fwd = np.zeros((P, 4, P), np.float32)
    rev = np.zeros((P, 4, P), np.float32)
    far = np.concatenate([w0[:, f, partner(4, 0)].T] * 3)
    w1s = x["L0_rec_W1"].reshape(P, 2, F, F)
    w1 = np.zeros((P, 16, P), np.float32)
    for q in range(4):
        rows = slice(F * q, F * q + F)
        for k in range(8):
            if k < 4:
                fwd[rows, k, :] = w0[:, f, partner(k, q)].T
            if k < 4 and k + q > 0:
                rev[rows, k, :] = w0[:, partner(k, q), f].T
            for way in range(2):
                w1[rows, way * 8 + k, :] = w1s[:, (q + way) % 2, f, partner(k, q)].T
    wt1 = x["W_top1"]
    nd = x["dense_ctx"].shape[1]
    wt1a = np.zeros((P, wt1.shape[1]), np.float32)
    wt1a[0:nd] = wt1[192:192 + nd]
    wt1a[64:128] = wt1[0:64]
    dense = np.zeros((64, B), np.float32)
    dense[0:nd] = x["dense_ctx"].T
    arrays = {
        "ids": x["ids"].reshape(G, P, F).transpose(1, 0, 2).reshape(P, G * F),
        "ident": np.eye(P, dtype=np.float32),
        "w0_fwd": fwd, "w0_rev": rev, "w0_far": far, "w1": w1,
        "b0": x["L0_rec_b0"].reshape(P, 1), "b1": x["L0_rec_b1"].reshape(P, 1),
        "dense": dense, "wt1a": wt1a, "wt1b": wt1[64:192],
        "bt1": x["b_top1"].reshape(4, P).T,
        "wt2": x["W_top2"].reshape(4, P, 256).transpose(1, 0, 2),
        "bt2": x["b_top2"].reshape(2, P).T,
        "wt3": x["W_top3"].reshape(2, P).T,
    }
    names = list(arrays)
    for i in range(F):
        arrays[f"tbl_{i}"] = x[f"tbl_{i}"]
    nc = _bacc.Bacc("TRN2", target_bir_lowering=False, num_devices=1)
    aps, feed = {}, {}
    for name, a in arrays.items():
        a = np.ascontiguousarray(a)
        feed[f"in_{name}_dram"] = a
        aps[name] = nc.dram_tensor(f"in_{name}_dram", a.shape, mybir.dt.from_np(a.dtype), kind="ExternalInput").ap()
    y = nc.dram_tensor("out_0_dram", (B, 1), mybir.dt.float32, kind="ExternalOutput").ap()
    cin_tower_program(nc, *[aps[n] for n in names], [aps[f"tbl_{i}"] for i in range(F)], y)
    r = _run(nc, [feed], core_ids=[0])
    return r.results[0]["out_0_dram"]
```
